# Optimizing a Trainium2 kernel written in Bass

```python
import numpy as np
import jax
import jax.numpy as jnp

def _softmax(x, axis=-1):
    return jax.nn.softmax(x, axis=axis)

def _gelu(x):
    return jax.nn.gelu(x, approximate=True)

def _silu(x):
    return jax.nn.silu(x)

def _sigmoid(x):
    return jax.nn.sigmoid(x)

def _layernorm(x, axis=-1, eps=1e-05):
    m = jnp.mean(x, axis=axis, keepdims=True)
    v = jnp.var(x, axis=axis, keepdims=True)
    return (x - m) / jnp.sqrt(v + eps)

def _scatter_add(tgt, idx, src, axis=0):
    return tgt.at[idx].add(src)

def _segment_sum(src, seg, n):
    return jax.ops.segment_sum(src, seg, n)
kernel_name = 'mk_lm_tower_d1_tok_ids256_r4_ffdf00'

def setup_inputs(seed: int=0):
    np.random.seed(seed)
    _w = jnp.asarray

    def _rec_inputs():
        import jax
        import jax.numpy as jnp
        _rk = jax.random.key(seed)
        x = jax.random.randint(jax.random.fold_in(_rk, 1), (2, 2048), 0, 75, jnp.int32)
        mask_BS_i0_1 = jnp.where(jnp.ones((2, 2048), dtype=bool), 0, 1).astype(jnp.int32)
        itok_BS_0_299 = jax.random.randint(jax.random.fold_in(_rk, 22), (2, 2048), 0, 75, jnp.int32)
        return (x, mask_BS_i0_1, itok_BS_0_299)
    x, mask_BS_i0_1, itok_BS_0_299 = _rec_inputs()

    def _L0_tok_setup():
        import jax, jax.numpy as jnp
        import numpy as np
        NUM_SKILLS = 75
        EMB_SIZE = 64
        CURVE_DIM = 64
        B, S = (128, 200)

        def _running_counts(q, r):
            b, s = q.shape
            rows = jnp.arange(b)
            valid = (q >= 0) & (q < NUM_SKILLS)
            idx = jnp.clip(q, 0, NUM_SKILLS - 1)

            def step(carry, xs):
                att, cor = carry
                it, rt, vt = xs
                att = att.at[rows, it].add(vt.astype(jnp.int32))
                cor = cor.at[rows, it].add((rt * vt).astype(jnp.int32))
                return ((att, cor), (att[rows, it], cor[rows, it]))
            init = (jnp.zeros((b, NUM_SKILLS), jnp.int32), jnp.zeros((b, NUM_SKILLS), jnp.int32))
            xs = (idx.T, r.T, valid.T)
            _, (a_t, c_t) = jax.lax.scan(step, init, xs)
            return (a_t.T.astype(jnp.float32), c_t.T.astype(jnp.float32), valid)
        key = jax.random.key(seed)
        ks = jax.random.split(key, 11)
        d3 = CURVE_DIM // 3
        dm = d3 + CURVE_DIM % 3
        return {'q': jax.random.randint(ks[0], (B, S), 0, NUM_SKILLS, dtype=jnp.int32), 'r': jax.random.randint(ks[1], (B, S), 0, 2, dtype=jnp.int32), 'qry': jax.random.randint(ks[2], (B, S), 0, NUM_SKILLS, dtype=jnp.int32), 'skill_w': jax.random.normal(ks[3], (d3,), jnp.float32), 'skill_b': jax.random.normal(ks[4], (d3,), jnp.float32), 'att_w': jax.random.normal(ks[5], (d3,), jnp.float32), 'att_b': jax.random.normal(ks[6], (d3,), jnp.float32), 'mast_w': jax.random.normal(ks[7], (dm,), jnp.float32), 'mast_b': jax.random.normal(ks[8], (dm,), jnp.float32), 'proj_w': jax.random.normal(ks[9], (EMB_SIZE, CURVE_DIM), jnp.float32) * 0.05, 'proj_b': jax.random.normal(ks[10], (EMB_SIZE,), jnp.float32)}
    _L0_tok_all = _L0_tok_setup()
    _L0_tok_in = {k: v for k, v in _L0_tok_all.items() if k in ('skill_w', 'skill_b', 'att_w', 'att_b', 'mast_w', 'mast_b', 'proj_w', 'proj_b')}
    del _L0_tok_all

    def _L0_attn_setup():
        import jax, jax.numpy as jnp
        import numpy as np
        B, S, DIM = (8, 1024, 64)
        DI, K, N, R = (128, 2, 16, 16)
        key = jax.random.key(seed)
        ks = jax.random.split(key, 10)
        s = 0.02
        return {'x': jax.random.normal(ks[0], (B, S, DIM), jnp.float32), 'W_in': jax.random.normal(ks[1], (2 * DI, DIM), jnp.float32) * s, 'conv_w': jax.random.normal(ks[2], (DI, DI), jnp.float32) * s, 'conv_b': jax.random.normal(ks[3], (DI,), jnp.float32) * s, 'x_proj_w': jax.random.normal(ks[4], (K, R + 2 * N, DI), jnp.float32) * s, 'dt_w': jax.random.normal(ks[5], (K, DI, R), jnp.float32) * s, 'dt_b': jax.random.normal(ks[6], (K, DI), jnp.float32) * s, 'A_logs': jax.random.uniform(ks[7], (K * DI, N), jnp.float32), 'Ds': jnp.ones((K * DI,), jnp.float32), 'ln_w': jnp.ones((DI,), jnp.float32), 'ln_b': jnp.zeros((DI,), jnp.float32), 'W_out': jax.random.normal(ks[8], (DIM, DI), jnp.float32) * s}
    _L0_attn_all = _L0_attn_setup()
    _L0_attn_in = {k: v for k, v in _L0_attn_all.items() if k in ('W_in', 'conv_w', 'conv_b', 'x_proj_w', 'dt_w', 'dt_b', 'A_logs', 'Ds', 'ln_w', 'ln_b', 'W_out')}
    del _L0_attn_all

    def _L0_ffn_setup():
        import jax, jax.numpy as jnp
        import numpy as np
        B, T, IN_DIM = (64, 64, 64)
        HID, OUT_DIM = (128, 64)
        N_LAYERS, N_EXPERTS, N_SHARED = (2, 16, 1)
        key = jax.random.key(seed)
        ks = jax.random.split(key, 10)
        s = 0.02
        x = jax.random.normal(ks[0], (B, T, IN_DIM), dtype=jnp.float32)
        route_id = jax.random.randint(ks[1], (B,), 0, N_EXPERTS)
        Wi = jax.random.normal(ks[2], (HID, IN_DIM), dtype=jnp.float32) * s
        bi = jnp.zeros((HID,), dtype=jnp.float32)
        Wr = jax.random.normal(ks[3], (N_LAYERS, N_EXPERTS, HID, HID), dtype=jnp.float32) * s
        br = jax.random.normal(ks[4], (N_LAYERS, N_EXPERTS, HID), dtype=jnp.float32) * s
        Ws = jax.random.normal(ks[5], (N_LAYERS, N_SHARED, HID, HID), dtype=jnp.float32) * s
        bs = jax.random.normal(ks[6], (N_LAYERS, N_SHARED, HID), dtype=jnp.float32) * s
        Wo = jax.random.normal(ks[7], (OUT_DIM, HID), dtype=jnp.float32) * s
        bo = jnp.zeros((OUT_DIM,), dtype=jnp.float32)
        return {'x': x, 'route_id': route_id, 'Wi': Wi, 'bi': bi, 'Wr': Wr, 'br': br, 'Ws': Ws, 'bs': bs, 'Wo': Wo, 'bo': bo}
    _L0_ffn_all = _L0_ffn_setup()
    _L0_ffn_in = {k: v for k, v in _L0_ffn_all.items() if k in ('route_id', 'Wi', 'bi', 'Wr', 'br', 'Ws', 'bs', 'Wo', 'bo')}
    del _L0_ffn_all
    return {'x': x, 'mask_BS_i0_1': mask_BS_i0_1, 'itok_BS_0_299': itok_BS_0_299, 'L0_tok_skill_w': _L0_tok_in['skill_w'], 'L0_tok_skill_b': _L0_tok_in['skill_b'], 'L0_tok_att_w': _L0_tok_in['att_w'], 'L0_tok_att_b': _L0_tok_in['att_b'], 'L0_tok_mast_w': _L0_tok_in['mast_w'], 'L0_tok_mast_b': _L0_tok_in['mast_b'], 'L0_tok_proj_w': _L0_tok_in['proj_w'], 'L0_tok_proj_b': _L0_tok_in['proj_b'], 'L0_attn_W_in': _L0_attn_in['W_in'], 'L0_attn_conv_w': _L0_attn_in['conv_w'], 'L0_attn_conv_b': _L0_attn_in['conv_b'], 'L0_attn_x_proj_w': _L0_attn_in['x_proj_w'], 'L0_attn_dt_w': _L0_attn_in['dt_w'], 'L0_attn_dt_b': _L0_attn_in['dt_b'], 'L0_attn_A_logs': _L0_attn_in['A_logs'], 'L0_attn_Ds': _L0_attn_in['Ds'], 'L0_attn_ln_w': _L0_attn_in['ln_w'], 'L0_attn_ln_b': _L0_attn_in['ln_b'], 'L0_attn_W_out': _L0_attn_in['W_out'], 'L0_ffn_route_id': _L0_ffn_in['route_id'], 'L0_ffn_Wi': _L0_ffn_in['Wi'], 'L0_ffn_bi': _L0_ffn_in['bi'], 'L0_ffn_Wr': _L0_ffn_in['Wr'], 'L0_ffn_br': _L0_ffn_in['br'], 'L0_ffn_Ws': _L0_ffn_in['Ws'], 'L0_ffn_bs': _L0_ffn_in['bs'], 'L0_ffn_Wo': _L0_ffn_in['Wo'], 'L0_ffn_bo': _L0_ffn_in['bo']}

def reference(x, mask_BS_i0_1, itok_BS_0_299, L0_tok_skill_w, L0_tok_skill_b, L0_tok_att_w, L0_tok_att_b, L0_tok_mast_w, L0_tok_mast_b, L0_tok_proj_w, L0_tok_proj_b, L0_attn_W_in, L0_attn_conv_w, L0_attn_conv_b, L0_attn_x_proj_w, L0_attn_dt_w, L0_attn_dt_b, L0_attn_A_logs, L0_attn_Ds, L0_attn_ln_w, L0_attn_ln_b, L0_attn_W_out, L0_ffn_route_id, L0_ffn_Wi, L0_ffn_bi, L0_ffn_Wr, L0_ffn_br, L0_ffn_Ws, L0_ffn_bs, L0_ffn_Wo, L0_ffn_bo):
    import jax
    import jax.numpy as jnp

    def _L0_tok_ref(q, r, qry, skill_w, skill_b, att_w, att_b, mast_w, mast_b, proj_w, proj_b):
        import jax, jax.numpy as jnp
        import numpy as np
        NUM_SKILLS = 75
        EMB_SIZE = 64
        CURVE_DIM = 64
        B, S = (128, 200)

        def _running_counts(q, r):
            b, s = q.shape
            rows = jnp.arange(b)
            valid = (q >= 0) & (q < NUM_SKILLS)
            idx = jnp.clip(q, 0, NUM_SKILLS - 1)

            def step(carry, xs):
                att, cor = carry
                it, rt, vt = xs
                att = att.at[rows, it].add(vt.astype(jnp.int32))
                cor = cor.at[rows, it].add((rt * vt).astype(jnp.int32))
                return ((att, cor), (att[rows, it], cor[rows, it]))
            init = (jnp.zeros((b, NUM_SKILLS), jnp.int32), jnp.zeros((b, NUM_SKILLS), jnp.int32))
            xs = (idx.T, r.T, valid.T)
            _, (a_t, c_t) = jax.lax.scan(step, init, xs)
            return (a_t.T.astype(jnp.float32), c_t.T.astype(jnp.float32), valid)
        attempts, correct, valid = _running_counts(q, r)
        mastery = correct / jnp.maximum(attempts, 1.0)
        skill_f = q.astype(jnp.float32)
        s_enc = skill_f[..., None] * skill_w + skill_b
        n_enc = attempts[..., None] * att_w + att_b
        m_enc = mastery[..., None] * mast_w + mast_b
        tup = jnp.concatenate([s_enc, n_enc, m_enc], axis=-1)
        traj = jnp.einsum('bsc,ec->bse', tup, proj_w) + proj_b
        return jnp.where(valid[..., None], traj, 0.0)

    def _L0_attn_ref(x, W_in, conv_w, conv_b, x_proj_w, dt_w, dt_b, A_logs, Ds, ln_w, ln_b, W_out):
        import jax, jax.numpy as jnp
        import numpy as np
        B, S, DIM = (8, 1024, 64)
        DI, K, N, R = (128, 2, 16, 16)
        Bb, L, dim = x.shape
        K_, DI_, R_ = dt_w.shape
        N_ = A_logs.shape[-1]
        xz = x @ W_in.T
        xx, z = jnp.split(xz, 2, axis=-1)
        z = jax.nn.silu(z)
        xx = jnp.einsum('ed,bld->bel', conv_w, xx) + conv_b[None, :, None]
        xx = jax.nn.silu(xx)
        xs = jnp.stack([xx, jnp.flip(xx, axis=-1)], axis=1)
        x_dbl = jnp.einsum('bkdl,kcd->bkcl', xs, x_proj_w)
        dts, Bs, Cs = jnp.split(x_dbl, [R_, R_ + N_], axis=2)
        dts = jnp.einsum('bkrl,kdr->bkdl', dts, dt_w)
        A = -jnp.exp(A_logs.astype(jnp.float32)).reshape(K_, DI_, N_)
        Dvec = Ds.astype(jnp.float32).reshape(K_, DI_)
        delta = jax.nn.softplus(dts + dt_b[None, :, :, None])
        dT = jnp.moveaxis(delta, -1, 0)
        uT = jnp.moveaxis(xs, -1, 0)
        BsT = jnp.moveaxis(Bs, -1, 0)
        CsT = jnp.moveaxis(Cs, -1, 0)

        def step(h, inp):
            dt, ut, bt, ct = inp
            h = jnp.exp(dt[..., None] * A) * h + (dt * ut)[..., None] * bt[:, :, None, :]
            y = jnp.einsum('bkdn,bkn->bkd', h, ct)
            return (h, y)
        h0 = jnp.zeros((Bb, K_, DI_, N_), jnp.float32)
        _, ysT = jax.lax.scan(step, h0, (dT, uT, BsT, CsT))
        out_y = jnp.moveaxis(ysT, 0, -1) + Dvec[None, :, :, None] * xs
        y = out_y[:, 0] + jnp.flip(out_y[:, 1], axis=-1)
        y = jnp.swapaxes(y, 1, 2)
        mu = y.mean(-1, keepdims=True)
        var = y.var(-1, keepdims=True)
        y = (y - mu) / jnp.sqrt(var + 1e-05) * ln_w + ln_b
        y = y * z
        return y @ W_out.T

    def _L0_ffn_ref(x, route_id, Wi, bi, Wr, br, Ws, bs, Wo, bo):
        import jax, jax.numpy as jnp
        import numpy as np
        B, T, IN_DIM = (64, 64, 64)
        HID, OUT_DIM = (128, 64)
        N_LAYERS, N_EXPERTS, N_SHARED = (2, 16, 1)
        flat = x.reshape(-1, x.shape[-1])
        n_tok = flat.shape[0]
        route = jnp.repeat(route_id, n_tok // route_id.shape[0])
        h = jax.nn.relu(flat @ Wi.T + bi)
        n_layers, n_experts = (Wr.shape[0], Wr.shape[1])
        for l in range(n_layers):
            shared = (jnp.einsum('nd,shd->snh', h, Ws[l]) + bs[l][:, None, :]).mean(axis=0)
            routed = jnp.zeros_like(h)
            for e in range(n_experts):
                ye = h @ Wr[l, e].T + br[l, e]
                routed = routed + jnp.where((route == e)[:, None], ye, 0.0)
            h = jax.nn.relu(shared + routed + h)
        out = h @ Wo.T + bo
        return out.reshape(*x.shape[:-1], out.shape[-1])
    h = _L0_tok_ref(x, mask_BS_i0_1, itok_BS_0_299, L0_tok_skill_w, L0_tok_skill_b, L0_tok_att_w, L0_tok_att_b, L0_tok_mast_w, L0_tok_mast_b, L0_tok_proj_w, L0_tok_proj_b)
    h = h + _L0_attn_ref(_layernorm(h, axis=-1), L0_attn_W_in, L0_attn_conv_w, L0_attn_conv_b, L0_attn_x_proj_w, L0_attn_dt_w, L0_attn_dt_b, L0_attn_A_logs, L0_attn_Ds, L0_attn_ln_w, L0_attn_ln_b, L0_attn_W_out)
    h = h + _L0_ffn_ref(_layernorm(h, axis=-1), L0_ffn_route_id, L0_ffn_Wi, L0_ffn_bi, L0_ffn_Wr, L0_ffn_br, L0_ffn_Ws, L0_ffn_bs, L0_ffn_Wo, L0_ffn_bo)
    return h

_drawn_inputs = setup_inputs


def setup_inputs(seed=0):
    import zlib

    import numpy as np

    out = dict(_drawn_inputs(seed))
    spreads = {'L0_attn_Ds': (1.0, 0.6),
     'L0_attn_ln_w': (1.0, 0.6),
     'L0_attn_ln_b': (0.0, 0.8),
     'L0_ffn_bi': (0.0, 0.8),
     'L0_ffn_bo': (0.0, 0.8)}
    factors = {'L0_tok_skill_b': 3.161,
     'L0_tok_att_b': 3.801,
     'L0_tok_mast_b': 3.344,
     'L0_attn_W_in': 8.0,
     'L0_attn_conv_w': 8.0,
     'L0_attn_conv_b': 8.0,
     'L0_attn_x_proj_w': 8.0,
     'L0_attn_dt_w': 8.0,
     'L0_attn_dt_b': 8.0,
     'L0_attn_A_logs': 8.0,
     'L0_attn_W_out': 8.0,
     'L0_ffn_Wi': 8.0,
     'L0_ffn_Wr': 8.0,
     'L0_ffn_br': 8.0,
     'L0_ffn_Ws': 8.0,
     'L0_ffn_bs': 8.0,
     'L0_ffn_Wo': 8.0}
    for name, (base, spread) in spreads.items():
        noise = np.random.default_rng([zlib.crc32(name.encode()), seed]).standard_normal(out[name].shape)
        drawn = base * np.exp(spread * noise) if base else spread * noise
        out[name] = jnp.asarray(drawn.astype(out[name].dtype))
    for name, factor in factors.items():
        out[name] = (out[name] * factor).astype(out[name].dtype)
    return out
```

```python
from contextlib import ExitStack

import concourse.bass as bass
from concourse import mybir

F32 = mybir.dt.float32
BF16 = mybir.dt.bfloat16
I32 = mybir.dt.int32
U16 = mybir.dt.uint16
ALU = mybir.AluOpType
ACT = mybir.ActivationFunctionType
AX = mybir.AxisListType
ds = bass.ds

B, L = 2, 2048
NSK = 75
E = 64
DI = 128
K = 2
N = 16
R = 16
HID = 128
NX = 16
NL = 2
NR = 64
TG = B * L // NR
T = B * L
NC = T // 128
CB = L // 128
CH = 1024
HC = 512
SL = 256
NSEG = B * K * (L // CH)
UN = 4
IT = N // UN
NF = 4
FR = 3 * 3 * NF
BCR = 112
EPS = 1e-5
BIG = 1e17
Q = T // HC
GQ = HC // TG

CF = {}
_at = 0
for _n, _w in (("ident", 128), ("tri", 128), ("cen128", 128), ("one128", 128), ("cen64", 128), ("one64", 128),
               ("iota", NSK), ("blk", NC), ("m36", 2), ("mbc", 2), ("m51", 2), ("eid", 2), ("ind", CB * CB), ("sel", 2 * N)):
    CF[_n] = (_at, _at + _w)
    _at += _w
CFW = _at
CHN = ["conv_b", "dt_b0", "dt_b1", "d0", "d1", "ln_w", "ln_b", "bi", "bo"]


def segment(s):
    b, r = divmod(s, 4)
    return b, (0, 0, 1, 1)[r], (0, 1, 1, 0)[r]


def bass_lm_tower(nc, tok, consts, cmask, chan, tokm, projt, wint, convt, xbc, xdt, dtw, alog, wout, wit, ws, wo,
                  wr, brb, route, routeb, scratch, out):
    with ExitStack() as ctx:
        def sb(name, shape, dt=F32):
            return ctx.enter_context(nc.sbuf_tensor(name, shape, dt))

        def sem(name):
            return ctx.enter_context(nc.semaphore(name))

        ps = ctx.enter_context(nc.psum_tensor("ps", [128, 8, 512], F32))

        cf = sb("cf", [128, CFW])
        cm = sb("cm", [CB, CB * 128])
        ch = sb("ch", [128, len(CHN)])
        tm = sb("tm", [E + 1, FR + 128])
        pt = sb("pt", [E + 1, 128])
        ptc = sb("ptc", [E + 1, E])
        pmean = sb("pmean", [E + 1, 2])
        win = sb("win", [E, 2 * DI])
        cvt = sb("cvt", [DI, DI])
        xb = sb("xb", [DI, K, BCR])
        xd = sb("xd", [R, K, DI])
        dw = sb("dw", [R, K, DI])
        wdt = sb("wdt", [DI, K, DI])
        al = sb("al", [DI, K * N])
        na = sb("na", [DI, K * N])
        wou = sb("wou", [DI, 128])
        wi_ = sb("wi_", [E, HID])
        si = sb("si", [HID, NL, HID])
        wo_ = sb("wo_", [HID, E])
        BR = 3 * (NX + 1)
        br = sb("br", [BR, NL * HID])
        brr = sb("brr", [BR, NL * HID])
        brh = sb("brh", [BR, NL * HID], BF16)
        brp = sb("brp", [BR, NL * HID], BF16)
        rtb = sb("rtb", [BR, NR], I32)
        ohr = sb("ohr", [BR, NR], BF16)
        rt = sb("rt", [1, NR], I32)
        rtw = sb("rtw", [1, 4, NR])
        slot = sb("slot", [1, NR], I32)
        selb = sb("selb", [128, 2 * N, 128], BF16)
        dsum = sb("dsum", [DI, 1])
        eps = sb("eps", [128, 1])
        ysv = sb("ysv", [DI, CH])

        tk = sb("tk", [128, 2, NC], I32)
        tf = sb("tf", [128, 2, NC])
        trib = sb("trib", [128, 128], BF16)
        indb = sb("indb", [128, CB * CB], BF16)
        cmb = sb("cmb", [CB, CB * 128], BF16)
        idb = sb("idb", [128, 128], BF16)
        tot = sb("tot", [CB, B * NSK], BF16)
        totr = sb("totr", [CB, B * NSK])
        f2 = sb("f2", [128, 2, NF * NC])
        ft = f2[:, 0, :].rearrange("p (f c) -> p f c", f=NF)
        ftn = f2[:, 1, :].rearrange("p (f c) -> p f c", f=NF)
        val = sb("val", [128, 3, NC])
        ftt = sb("ftt", [128, 128])
        ss = sb("ss", [128, 3, NC])
        parts = sb("parts", [128, 3, 2, 128], BF16)
        rest = sb("rest", [128, 2, 128])
        fts = sb("fts", [128, 6, 128], BF16)
        bdc = sb("bdc", [128, NC, E])
        wrc = sb("wrc", [128, E])
        w2 = sb("w2", [E, FR])
        gx = sb("gx", [DI, FR])
        GC = 3 * 128
        gwr = sb("gwr", [FR, GC])
        gwh = sb("gwh", [FR, 2, GC], BF16)
        g36 = sb("g36", [FR, GC], BF16)
        f36 = sb("f36", [FR, 2, T], BF16)

        u = sb("u", [DI, T])
        z = sb("z", [DI, T])
        dl = sb("dl", [DI, 2, CH])
        du = sb("du", [DI, 2, CH])
        pr = sb("pr", [BCR, 2, CH], BF16)
        xe = sb("xe", [DI, CH])
        xl = sb("xl", [DI, CH])
        xh = sb("xh", [BCR, CH], BF16)
        xr = sb("xr", [BCR, CH])
        xm = sb("xm", [BCR, CH], BF16)
        carry = sb("carry", [DI, N])
        AR = 4
        big = sb("big", [128, AR * HC + 3 * UN * CH])
        oh = big[:, 0:1200].bitcast(BF16).rearrange("p (c b s) -> p c b s", c=CB, b=B)
        ohq = big[:, 1200:3600].rearrange("p (c b s) -> p c b s", c=CB, b=B)
        prod = big[:, 3600:8400].rearrange("p (w c b s) -> p w c b s", w=2, c=CB, b=B)
        hsq = big[:, 8400:8400 + NC * E].rearrange("p (c e) -> p c e", c=NC)
        av = big[:, 0:AR * HC].rearrange("p (r t) -> p r t", r=AR)
        o = AR * HC
        hv, cv, pv = (big[:, o + w * UN * CH:o + (w + 1) * UN * CH].rearrange("p (r t) -> p r t", r=UN)
                      for w in range(3))
        sq, rs, tt, hn, fa, fb, h1, ot = (big[:, 2 * HC * w:2 * HC * (w + 1)].rearrange("p (r t) -> p r t", r=2)
                                          for w in range(8))
        we = big[:, 16 * HC:16 * HC + 2 * GQ * NL * HID].rearrange("p (r l j) -> p r l j", r=2 * GQ, l=NL)

        s_tok, s_con, s_cm, s_w, s_late = (sem(n) for n in (
            "tok_loaded", "consts_loaded", "cmask_loaded", "weights_loaded", "late_loaded"))
        s_scr, s_f36 = sem("parts_in_dram"), sem("features_loaded")
        casts, sel_ready, neg_a, exp_a = sem("casts"), sem("sel_ready"), sem("neg_a"), sem("exp_a")
        proj_c, set1, set1_sb, set2, set2_sb, set3 = (sem(n) for n in (
            "proj_centred", "setup1", "setup1_copied", "setup2", "setup2_copied", "setup3"))
        g_step, bias_step, route_step, dsum_ready, bdc_ready, si_ready = (sem(n) for n in (
            "g_step", "bias_step", "route_step", "dsum_ready", "bdc_ready", "si_ready"))
        tok_f, onehot, onehot_r, tot_ready, tot_sb, cum_ready, cum_used = (sem(n) for n in (
            "tok_float", "onehot", "onehot_r", "totals", "totals_copied", "cum_ready", "cum_used"))
        feat, ft_ready, ft_sb, hc_ready, hsq_ready, ss_ready, rstd_ready = (sem(n) for n in (
            "features", "features_t", "features_t_copied", "h_centred", "h_squared", "ss_ready", "rstd_ready"))
        ss_step, eps_set = sem("ss_step"), sem("eps_set")
        part_step, fts_ready, fts_sb = sem("part_step"), sem("parts_t"), sem("parts_t_copied")
        xz_ready, xz_done = sem("xz_ready"), sem("xz_done")
        x_ready, x_exp, x_hi, x_min, x_rest, x_ln, x_mid, x_parts, x_delta, x_du = (sem(n) for n in (
            "x_ready", "x_exp", "x_hi", "x_min", "x_rest", "x_ln", "x_mid", "x_parts", "x_delta", "x_du"))
        b_ready, c_ready, c_copied, a_ready, mul_done, scan_done = (sem(n) for n in (
            "b_ready", "c_ready", "c_copied", "a_ready", "mul_done", "scan_done"))
        carry_saved, p_done, sum_done, y_taken = (sem(n) for n in (
            "carry_saved", "p_done", "sum_done", "y_taken"))
        q_yc, q_sq, q_var, q_ln, q_rs, q_t1, q_t, q_o, q_h1, q_hc = (sem(n) for n in (
            "y_centred", "y_squared", "y_var", "y_ln", "y_rstd", "y_scaled", "y_gated",
            "o_ready", "h1_ready", "h1_centred"))
        q_sq2, q_var2, q_ln2, q_rs2, q_hn, q_w, q_f0, q_l0, q_f1, q_l1, q_f2, q_wo, q_out = (
            sem(n) for n in ("h1_squared", "h1_var", "h1_ln", "h1_rstd", "h1_normed", "wi_ready", "f0_ready",
                             "l0_ready", "f1_ready", "l1_ready", "f2_ready", "wo_ready", "out_ready"))
        we_loaded = [sem(f"experts_loaded{p}") for p in range(2)]
        out_stored = [sem(f"out_stored{p}") for p in range(2)]

        def con(name, rows=128):
            a, b_ = CF[name]
            return cf[0:rows, a:b_]

        def chn(name, rows=128):
            i = CHN.index(name)
            return ch[0:rows, i:i + 1]

        def cb_view(ap):
            return ap.rearrange("p (b c) -> p c b", b=B)

        def prepared(s, it):
            return it if s == 0 else 2 + (s - 1) * IT + it

        def slice_at(s, it):
            b, k, c = segment(s)
            return b * L + c * CH + (it * SL if k == 0 else it * -SL + (IT - 1) * SL)

        def phys(k, h):
            return h if k == 0 else 1 - h

        def opt_ge(eng, s, v, ok):
            if ok:
                eng.wait_ge(s, v)

        def snapped(eng, v):
            return v if isinstance(v, int) else eng.snap(v)

        block = ctx.enter_context(nc.Block())

        @block.sync
        def _(sp):
            sp.dma_start(tk[:], tok).then_inc(s_tok, 16)
            sp.dma_start(cf[:], consts).then_inc(s_con, 16)
            sp.dma_start(cm[:], cmask).then_inc(s_cm, 16)
            for dst, src in ((al, alog), (wou, wout), (wi_, wit), (si, ws), (wo_, wo), (br, brb), (rtb, routeb),
                             (rt, route)):
                sp.dma_start(dst[:], src).then_inc(s_late, 16)
            sp.wait_ge(fts_sb, 1)
            sp.dma_start(scratch.rearrange("v i p t -> p (v i) t"), fts[:]).then_inc(s_scr, 16)
            sp.wait_ge(s_scr, 16)
            for v in range(2):
                for j in range(3):
                    sp.dma_start(f36[12 * j:12 * j + 12, v, :],
                                 scratch[v].rearrange("i (f c) t -> (i f) (c t)", f=NF)).then_inc(s_f36, 16)

            def experts(q, p):
                for g in range(GQ):
                    e = sp.value_load(slot[0:1, ds(q * GQ + g, 1)], min_val=0, max_val=NX)
                    sp.dma_start(we[:, p * GQ + g, :, :], wr[ds(e, 1)].rearrange("o i l j -> i (o l) j")
                                 ).then_inc(we_loaded[p], 16)

            sp.wait_ge(route_step, 5)
            sp.wait_ge(sum_done, N * NSEG)
            for p in range(2):
                experts(p, p)
            with sp.Fori(0, Q // 2 - 1) as qq:
                for p in range(2):
                    sp.wait_ge(q_l1, 2 * qq + p + 1)
                    experts(2 * qq + p + 2, p)
                for p in range(2):
                    sp.wait_ge(q_out, 2 * qq + p + 1)
                    sp.dma_start(out[:, ds((2 * qq + p) * HC, HC)], ot[0:E, p, :]).then_inc(out_stored[p], 16)
            for q in (Q - 2, Q - 1):
                sp.wait_ge(q_out, q + 1)
                sp.dma_start(out[:, q * HC:(q + 1) * HC], ot[0:E, q % 2, :]).then_inc(out_stored[q % 2], 16)
            for p in range(2):
                sp.wait_ge(out_stored[p], 16 * Q // 2)

        @block.gpsimd
        def _(pool):
            pool.wait_ge(s_con, 16)
            pool.tensor_copy(indb[:], con("ind")).then_inc(casts, 1)
            pool.tensor_copy(trib[:], con("tri")).then_inc(casts, 1)
            pool.wait_ge(s_cm, 16)
            pool.tensor_copy(cmb[:], cm[:]).then_inc(casts, 1)
            pool.tensor_copy(idb[:], con("ident")).then_inc(casts, 1)
            pool.tensor_copy(selb[:], con("sel").unsqueeze(2).to_broadcast([128, 2 * N, 128])).then_inc(sel_ready, 1)

            def product(s, n, j, first):
                st = s * N + n
                pool.wait_ge(scan_done, 2 * st + 2)
                pool.wait_ge(c_copied, 2 * st + 2)
                opt_ge(pool, sum_done, st - UN + 1, not first)
                pool.tensor_tensor(pv[:, j, :], hv[:, j, :], cv[:, j, :], ALU.mult).then_inc(p_done, 1)

            for s in range(NSEG):
                for j in range(UN):
                    product(s, j, j, s == 0)
                with pool.Fori(1, IT) as it:
                    for j in range(UN):
                        product(s, it * UN + j, j, False)

        @block.scalar
        def _(act):
            for dst, src in ((tm, tokm), (pt, projt), (win, wint), (cvt, convt), (xb, xbc), (xd, xdt), (dw, dtw),
                             (ch, chan)):
                act.dma_start(dst[:], src).then_inc(s_w, 16)
            act.preload_act_table_set("natural_log_exp_and_others")
            act.wait_ge(set1, 1)
            act.activation(w2[:], ps[0:E, 6, 0:FR], ACT.Copy).then_inc(set1_sb, 1)
            act.activation(wrc[:], ps[:, 6, 64:128], ACT.Copy).then_inc(set1_sb, 1)
            act.activation(wdt[:], ps[:, 6, 256:512].rearrange("p (k d) -> p k d", k=K), ACT.Copy).then_inc(set1_sb, 1)
            act.wait_ge(set2, 1)
            act.activation(gx[:], ps[:, 6, 128:128 + FR], ACT.Copy).then_inc(set2_sb, 1)
            act.wait_ge(s_late, 16 * 8)
            act.activation(na[:], al[:], ACT.Exp).then_inc(exp_a, 1)
            act.wait_ge(exp_a, 1)
            act.activation(na[:], na[:], ACT.Copy, scale=-1.0).then_inc(neg_a, 1)
            act.wait_ge(tot_ready, 2)
            act.activation(tot[:], ps[0:CB, 0, 0:B * NSK], ACT.Copy).then_inc(tot_sb, 1)
            act.activation(totr[:], ps[0:CB, 0, 256:256 + B * NSK], ACT.Copy).then_inc(tot_sb, 1)
            act.wait_ge(ft_ready, 1)
            act.activation(ftt[:], ps[:, 0, 0:128], ACT.Copy).then_inc(ft_sb, 1)
            for i in range(4):
                act.wait_ge(hc_ready, i + 1)
                act.activation(hsq[:, 8 * i:8 * i + 8, :], ps[:, 1 + i, :].rearrange("p (c e) -> p c e", e=E),
                               ACT.Square).then_inc(hsq_ready, 1)
            act.wait_ge(ss_ready, 1)
            act.activation(ss[:, 2, :], ss[:, 1, :], ACT.Ln).then_inc(rstd_ready, 1)
            act.wait_ge(rstd_ready, 1)
            act.activation(ss[:, 0, :], ss[:, 2, :], ACT.Exp, scale=-0.5).then_inc(rstd_ready, 1)
            act.wait_ge(fts_ready, 1)
            act.activation(fts[:].rearrange("p i t -> p (i t)"), ps[:, 0, 0:384].bitcast(BF16), ACT.Copy
                           ).then_inc(fts_sb, 1)
            for w, (dst, bias) in enumerate(((u, chn("conv_b")), (z, 0.0))):
                with act.Fori(0, B) as b:
                    for i in range(4):
                        act.wait_ge(xz_ready, w * Q + b * 4 + i + 1)
                        act.activation(dst[:, ds(b * L + i * HC, HC)], ps[:, i, :], ACT.Silu, bias=bias
                                       ).then_inc(xz_done, 1)

            act.preload_act_table_set("natural_log_exp_and_others")

            def prep_exp(s, it, t0, width, bank, bc, o):
                _, k, _ = segment(s)
                act.wait_ge(x_ready, prepared(s, it) + 1)
                act.activation(xe[:, o:o + width], bank[:, :], ACT.Exp, bias=chn(f"dt_b{k}")).then_inc(x_exp, 1)
                act.activation(xh[:, o:o + width], bc, ACT.Copy).then_inc(x_hi, 1)

            def prep_ln(s, it, width, o):
                act.wait_ge(x_min, prepared(s, it) + 1)
                act.activation(xl[:, o:o + width], xe[:, o:o + width], ACT.Ln, bias=1.0).then_inc(x_ln, 1)
                act.wait_ge(x_rest, prepared(s, it) + 1)
                act.activation(xm[:, o:o + width], xr[:, o:o + width], ACT.Copy).then_inc(x_mid, 1)

            for i in range(2):
                prep_exp(0, i, i * HC, HC, ps[:, 5 + 2 * i, :], ps[0:BCR, 4 + 2 * i, :], i * HC)
            for i in range(2):
                prep_ln(0, i, HC, i * HC)

            def state(s, n, j, first):
                _, k, _ = segment(s)
                for h in range(2):
                    st = s * N + n
                    g = 2 * st + h
                    t = phys(k, h) * HC
                    opt_ge(act, scan_done, g - AR + 1, not (first and 2 * j + h < AR))
                    act.wait_ge(c_ready, g + 1)
                    if h == 0:
                        opt_ge(act, p_done, st - UN + 1, not first)
                    act.activation(cv[:, j, t:t + HC], ps[:, 4 + h, :], ACT.Copy).then_inc(c_copied, 1)
                    act.activation(av[:, (2 * j + h) % AR, :], dl[:, s % 2, t:t + HC], ACT.Exp,
                                   scale=na[:, ds(k * N + n, 1)]).then_inc(a_ready, 1)

            def turn(s, it, first):
                for j in range(UN):
                    if j == 1 and s + 1 < NSEG:
                        prep_exp(s + 1, it, None, SL, ps[:, 6, SL:2 * SL], ps[0:BCR, 6, 0:SL], 0)
                    state(s, it * UN + j, j, first)
                    if j == 2 and s + 1 < NSEG:
                        prep_ln(s + 1, it, SL, 0)

            act.wait_ge(neg_a, 1)
            for s in range(NSEG):
                act.wait_ge(x_delta, prepared(s + 1, 0))
                turn(s, 0, s == 0)
                with act.Fori(1, IT) as it:
                    turn(s, it, False)

            def last(q, p):
                a, b_, c_, d = (4 * p + i for i in range(4))

                def s1():
                    act.wait_ge(q_yc, q + 1)
                    act.activation(sq[:, p, :], ps[:, a, :], ACT.Square).then_inc(q_sq, 1)

                def s2():
                    act.wait_ge(q_var, q + 1)
                    act.activation(rs[:, p, :], ps[:, b_, :], ACT.Ln, bias=eps[:, 0:1]).then_inc(q_ln, 1)

                def s3():
                    act.wait_ge(q_ln, q + 1)
                    act.activation(rs[:, p, :], rs[:, p, :], ACT.Exp, scale=-0.5).then_inc(q_rs, 1)

                def s4():
                    act.wait_ge(q_o, q + 1)
                    act.activation(h1[0:E, p, :], ps[0:E, c_, :], ACT.Copy).then_inc(q_h1, 1)

                def s5():
                    act.wait_ge(q_hc, q + 1)
                    act.activation(sq[0:E, p, :], ps[0:E, d, :], ACT.Square).then_inc(q_sq2, 1)

                def s6():
                    act.wait_ge(q_var2, q + 1)
                    act.activation(rs[0:E, p, :], ps[0:E, b_, :], ACT.Ln, bias=eps[0:E, 0:1]).then_inc(q_ln2, 1)

                def s7():
                    act.wait_ge(q_ln2, q + 1)
                    act.activation(rs[0:E, p, :], rs[0:E, p, :], ACT.Exp, scale=-0.5).then_inc(q_rs2, 1)

                def s8():
                    act.wait_ge(q_w, q + 1)
                    act.activation(fa[:, p, :], ps[:, a, :], ACT.Relu, bias=chn("bi")).then_inc(q_f0, 1)

                def s9():
                    act.wait_ge(q_l0, q + 1)
                    act.activation(fb[:, p, :], ps[:, c_, :], ACT.Relu).then_inc(q_f1, 1)

                def s10():
                    act.wait_ge(q_l1, q + 1)
                    act.activation(fa[:, p, :], ps[:, d, :], ACT.Relu).then_inc(q_f2, 1)

                return (s1, s2, s3, s4, s5, s6, s7, s8, s9, s10)

            with act.Fori(0, Q // 2) as qq:
                both = [last(2 * qq + p, p) for p in range(2)]
                for st in zip(*both):
                    for f in st:
                        f()

        @block.vector
        def _(dve):
            dve.memset(eps[:], EPS).then_inc(eps_set, 1)
            dve.wait_ge(s_tok, 16)
            dve.tensor_copy(tf[:], tk[:]).then_inc(tok_f, 1)
            dve.wait_ge(s_con, 16)
            dve.wait_ge(tok_f, 1)
            iot = con("iota").unsqueeze(1).unsqueeze(1).to_broadcast([128, CB, B, NSK])
            qv = cb_view(tf[:, 0, :]).unsqueeze(3).to_broadcast([128, CB, B, NSK])
            rv = cb_view(tf[:, 1, :]).unsqueeze(3).to_broadcast([128, CB, B, NSK])
            dve.tensor_tensor(oh, iot, qv, ALU.is_equal).then_inc(onehot, 1)
            dve.wait_ge(s_w, 16 * 8)
            dve.tensor_reduce(pmean[:, 0:1], pt[:, 0:E], AX.X, ALU.add).then_inc(proj_c, 1)
            dve.wait_ge(proj_c, 1)
            dve.tensor_scalar(pmean[:, 1:2], pmean[:, 0:1], -1.0 / E, None, ALU.mult).then_inc(proj_c, 1)
            dve.wait_ge(proj_c, 2)
            dve.tensor_scalar(ptc[:], pt[:, 0:E], pmean[:, 1:2], None, ALU.add).then_inc(proj_c, 1)
            dve.wait_ge(onehot, 1)
            dve.tensor_tensor(ohq, oh, rv, ALU.mult).then_inc(onehot_r, 1)
            dve.tensor_scalar(val[:, 0, :], tf[:, 0, :], 0.0, None, ALU.is_ge).then_inc(feat, 1)
            dve.wait_ge(feat, 1)
            dve.scalar_tensor_tensor(ft[:, 3, :], tf[:, 0, :], float(NSK), val[:, 0, :], ALU.is_lt, ALU.mult
                                     ).then_inc(feat, 1)
            dve.wait_ge(feat, 2)
            dve.tensor_tensor(ft[:, 0, :], tf[:, 0, :], ft[:, 3, :], ALU.mult).then_inc(feat, 1)
            dve.wait_ge(set1_sb, 2)
            dve.tensor_tensor(bdc[:], wrc[:].unsqueeze(1).to_broadcast([128, NC, E]),
                              con("blk").unsqueeze(2).to_broadcast([128, NC, E]), ALU.mult).then_inc(bdc_ready, 1)
            gp = ps[0:FR, 7, 0:GC]
            dve.wait_ge(set3, 1)
            dve.tensor_copy(gwh[:, 0, :], gp).then_inc(g_step, 1)
            dve.wait_ge(g_step, 1)
            dve.scalar_tensor_tensor(gwr[:], gwh[:, 0, :], con("m36", FR)[:, 0:1], gp, ALU.mult, ALU.add
                                     ).then_inc(g_step, 1)
            dve.wait_ge(g_step, 2)
            dve.tensor_copy(gwh[:, 1, :], gwr[:]).then_inc(g_step, 1)
            dve.wait_ge(g_step, 3)
            dve.scalar_tensor_tensor(g36[:], gwh[:, 1, :], con("m36", FR)[:, 1:2], gwr[:], ALU.mult, ALU.add
                                     ).then_inc(g_step, 1)
            for w in range(2):
                for i in range(6):
                    n = min(3, CB - 3 * i)
                    dve.wait_ge(cum_ready, 6 * w + i + 1)
                    dve.tensor_tensor(prod[:, w, 3 * i:3 * i + n].rearrange("p c b s -> p (c b s)"),
                                      ps[:, 1 + i, 0:n * B * NSK],
                                      oh[:, 3 * i:3 * i + n].rearrange("p c b s -> p (c b s)"), ALU.mult
                                      ).then_inc(cum_used, 1)
                if w == 0:
                    dve.wait_ge(cum_used, 6)
                    dve.tensor_reduce(cb_view(ft[:, 1, :]), prod[:, 0], AX.X, ALU.add).then_inc(feat, 1)
                    dve.wait_ge(feat, 4)
                    dve.tensor_scalar(val[:, 0, :], ft[:, 1, :], 1.0, None, ALU.max).then_inc(feat, 1)
                    dve.wait_ge(feat, 5)
                    dve.reciprocal(val[:, 1, :], val[:, 0, :]).then_inc(feat, 1)
            dve.wait_ge(cum_used, 12)
            dve.tensor_reduce(cb_view(val[:, 2, :]), prod[:, 1], AX.X, ALU.add).then_inc(feat, 1)
            dve.wait_ge(feat, 7)
            dve.tensor_tensor(ft[:, 2, :], val[:, 2, :], val[:, 1, :], ALU.mult).then_inc(feat, 1)
            dve.wait_ge(hsq_ready, 4)
            dve.tensor_reduce(ss[:, 0, :], hsq, AX.X, ALU.add).then_inc(ss_step, 1)
            dve.wait_ge(ss_step, 1)
            dve.tensor_scalar(ss[:, 1, :], ss[:, 0, :], 1.0 / E, EPS, ALU.mult, ALU.add).then_inc(ss_ready, 1)
            dve.wait_ge(rstd_ready, 2)
            dve.tensor_tensor(ftn, ft, ss[:, 0, :].unsqueeze(1).to_broadcast([128, NF, NC]), ALU.mult
                              ).then_inc(part_step, 1)
            dve.wait_ge(part_step, 1)
            dve.tensor_copy(parts[:, 0], f2[:]).then_inc(part_step, 1)
            dve.wait_ge(part_step, 2)
            dve.tensor_tensor(rest[:], f2[:], parts[:, 0], ALU.subtract).then_inc(part_step, 1)
            dve.wait_ge(part_step, 3)
            dve.tensor_copy(parts[:, 1], rest[:]).then_inc(part_step, 1)
            dve.wait_ge(part_step, 4)
            dve.tensor_tensor(parts[:, 2], rest[:], parts[:, 1], ALU.subtract).then_inc(part_step, 1)
            dve.wait_ge(s_late, 16 * 8)
            dve.tensor_tensor(dsum[:], chn("d0"), chn("d1"), ALU.add).then_inc(dsum_ready, 1)
            dve.tensor_tensor(si[:], si[:], con("ident").unsqueeze(1).to_broadcast([HID, NL, HID]), ALU.add
                              ).then_inc(si_ready, 1)
            dve.tensor_copy(brh[:], br[:]).then_inc(bias_step, 1)
            dve.wait_ge(bias_step, 1)
            dve.scalar_tensor_tensor(brr[:], brh[:], con("m51", BR)[:, 0:1], br[:], ALU.mult, ALU.add
                                     ).then_inc(bias_step, 1)
            dve.wait_ge(bias_step, 2)
            dve.tensor_copy(brh[:], brr[:]).then_inc(bias_step, 1)
            dve.wait_ge(bias_step, 3)
            dve.scalar_tensor_tensor(brp[:], brh[:], con("m51", BR)[:, 1:2], brr[:], ALU.mult, ALU.add
                                     ).then_inc(bias_step, 1)
            dve.tensor_scalar(ohr[:], rtb[:], con("eid", BR)[:, 0:1], con("eid", BR)[:, 1:2], ALU.is_equal, ALU.max
                              ).then_inc(bias_step, 1)
            dve.tensor_copy(rtw[:, 0, :], rt[:]).then_inc(route_step, 1)
            dve.wait_ge(route_step, 1)
            dve.tensor_scalar(rtw[:, 1, :], rtw[:, 0, :], 0.0, None, ALU.is_ge).then_inc(route_step, 1)
            dve.wait_ge(route_step, 2)
            dve.scalar_tensor_tensor(rtw[:, 2, :], rtw[:, 0, :], float(NX), rtw[:, 1, :], ALU.is_lt, ALU.mult
                                     ).then_inc(route_step, 1)
            dve.wait_ge(route_step, 3)
            dve.scalar_tensor_tensor(rtw[:, 3, :], rtw[:, 0, :], -float(NX), rtw[:, 2, :], ALU.add, ALU.mult
                                     ).then_inc(route_step, 1)
            dve.wait_ge(route_step, 4)
            dve.tensor_scalar(slot[:], rtw[:, 3, :], float(NX), None, ALU.add).then_inc(route_step, 1)

            def prep_a(s, it, width, bc, o):
                t = prepared(s, it)
                dve.wait_ge(x_exp, t + 1)
                dve.tensor_scalar(xe[:, o:o + width], xe[:, o:o + width], BIG, None, ALU.min).then_inc(x_min, 1)
                dve.wait_ge(x_hi, t + 1)
                dve.scalar_tensor_tensor(xr[:, o:o + width], xh[:, o:o + width], con("mbc", BCR)[:, 0:1], bc,
                                         ALU.mult, ALU.add).then_inc(x_rest, 1)

            def prep_b(s, it, width, bank, o, u_ap, r_ap):
                b, k, c = segment(s)
                t = prepared(s, it)
                dve.wait_ge(x_mid, t + 1)
                dve.wait_ge(x_rest, t + 1)
                dve.scalar_tensor_tensor(r_ap(pr), xm[:, o:o + width], con("mbc", BCR)[:, 1:2], xr[:, o:o + width],
                                         ALU.mult, ALU.add).then_inc(x_parts, 1)
                dve.wait_ge(x_ln, t + 1)
                dve.scalar_tensor_tensor(r_ap(dl), bank, chn(f"dt_b{k}"), xl[:, o:o + width], ALU.add, ALU.max
                                         ).then_inc(x_delta, 1)
                dve.wait_ge(x_delta, t + 1)
                dve.tensor_tensor(r_ap(du), r_ap(dl), u_ap, ALU.mult).then_inc(x_du, 1)

            for i in range(2):
                prep_a(0, i, HC, ps[0:BCR, 4 + 2 * i, :], i * HC)
            for i in range(2):
                prep_b(0, i, HC, ps[:, 5 + 2 * i, :], i * HC, u[:, i * HC:(i + 1) * HC],
                       lambda x: x[:, 0, i * HC:(i + 1) * HC])

            def state(s, n, j, first):
                b, k, c = segment(s)
                start = s % 2 == 0
                st = s * N + n
                for h in range(2):
                    g = 2 * st + h
                    t = phys(k, h) * HC

                    def way(ap):
                        return ap if k == 0 else ap[:, ::-1]

                    bank = ps[:, 2 + h, :]
                    dve.wait_ge(b_ready, g + 1)
                    dve.tensor_tensor(bank, bank, du[:, s % 2, t:t + HC], ALU.mult).then_inc(mul_done, 1)
                    if h == 0:
                        opt_ge(dve, p_done, st - UN + 1, not first)
                        initial = 0.0 if start else carry[:, ds(n, 1)]
                    else:
                        e = phys(k, 0) * HC + (HC - 1 if k == 0 else 0)
                        initial = hv[:, j, e:e + 1]
                        dve.wait_ge(scan_done, g)
                    dve.wait_ge(a_ready, g + 1)
                    dve.wait_ge(mul_done, g + 1)
                    dve.tensor_tensor_scan(way(hv[:, j, t:t + HC]), way(av[:, (2 * j + h) % AR, :]), way(bank),
                                           initial, ALU.mult, ALU.add).then_inc(scan_done, 1)
                if start:
                    e = CH - 1 if k == 0 else 0
                    dve.wait_ge(scan_done, 2 * st + 2)
                    dve.tensor_copy(carry[:, ds(n, 1)], hv[:, j, e:e + 1]).then_inc(carry_saved, 1)

            def take_y(s):
                b, k, c = segment(s)
                y = ps[:, 0:2, :].rearrange("p w t -> p (w t)")
                uc = u[:, b * L + c * CH:b * L + (c + 1) * CH]
                dve.wait_ge(sum_done, N * (s + 1))
                if s % 4 == 0:
                    ins = dve.scalar_tensor_tensor(ysv[:], uc, dsum[:, 0:1], y, ALU.mult, ALU.add)
                elif s % 4 == 2:
                    ins = dve.scalar_tensor_tensor(uc, uc, dsum[:, 0:1], y, ALU.mult, ALU.add)
                else:
                    ins = dve.tensor_tensor(uc, ysv[:], y, ALU.add)
                ins.then_inc(y_taken, 1)

            def turn(s, it, first):
                nx = s + 1
                if nx < NSEG:
                    nb, nk, nc_ = segment(nx)
                    local = snapped(dve, it * SL if nk == 0 else it * -SL + (IT - 1) * SL)
                for j in range(UN):
                    state(s, it * UN + j, j, first)
                    if first_turn(it) and j == 1 and s > 0 and (s - 1) % 4 != 1:
                        take_y(s - 1)
                    if j == 0 and nx < NSEG:
                        prep_a(nx, it, SL, ps[0:BCR, 6, 0:SL], 0)
                    if j == 2 and nx < NSEG:
                        prep_b(nx, it, SL, ps[:, 6, SL:2 * SL], 0,
                               u[:, ds(nb * L + nc_ * CH + local, SL)], lambda x: x[:, nx % 2, ds(local, SL)])

            def first_turn(it):
                return isinstance(it, int)

            for s in range(NSEG):
                dve.wait_ge(x_du, prepared(s + 1, 0))
                opt_ge(dve, c_ready, 2 * N * s, s > 0)
                turn(s, 0, s == 0)
                with dve.Fori(1, IT) as it:
                    turn(s, it, False)
            take_y(NSEG - 1)

            def last(qq, p):
                q = 2 * qq + p
                a, b_, c_, d = (4 * p + i for i in range(4))

                def s1():
                    dve.wait_ge(q_rs, q + 1)
                    dve.scalar_tensor_tensor(tt[:, p, :], ps[:, a, :], chn("ln_w"), rs[:, p, :], ALU.mult, ALU.mult
                                             ).then_inc(q_t1, 1)

                def s2():
                    dve.wait_ge(q_t1, q + 1)
                    dve.scalar_tensor_tensor(tt[:, p, :], tt[:, p, :], chn("ln_b"), z[:, ds(q * HC, HC)],
                                             ALU.add, ALU.mult).then_inc(q_t, 1)

                def s3():
                    dve.wait_ge(q_rs2, q + 1)
                    dve.tensor_tensor(hn[0:E, p, :], ps[0:E, d, :], rs[0:E, p, :], ALU.mult).then_inc(q_hn, 1)

                def s4():
                    dve.wait_ge(q_wo, q + 1)
                    opt_ge(dve, out_stored[p], 16 * qq, not isinstance(qq, int))
                    dve.scalar_tensor_tensor(ot[0:E, p, :], ps[0:E, b_, :], chn("bo", E), h1[0:E, p, :],
                                             ALU.add, ALU.add).then_inc(q_out, 1)

                return (s1, s2, s3, s4)

            both = [last(0, p) for p in range(2)]
            for st in zip(*both):
                for f in st:
                    f()
            with dve.Fori(1, Q // 2) as qq:
                both = [last(qq, p) for p in range(2)]
                for st in zip(*both):
                    for f in st:
                        f()

        @block.tensor
        def _(pe):
            pe.wait_ge(s_w, 16 * 8)
            pe.wait_ge(proj_c, 3)
            pe.matmul(ps[0:E, 6, 0:FR], ptc[:], tm[:, 0:FR], start=True, stop=True)
            pe.matmul(ps[:, 6, 64:128], tm[:, FR:FR + 128], ptc[:], start=True, stop=True)
            for k in range(K):
                last_mm = pe.matmul(ps[:, 6, 256 + k * DI:256 + (k + 1) * DI], xd[:, k, :], dw[:, k, :],
                                    start=True, stop=True)
            last_mm.then_inc(set1, 1)
            pe.matmul(ps[0:FR, 7, 0:128], tm[:, 0:FR], pt[:], start=True, stop=True)
            pe.wait_ge(set1_sb, 3)
            pe.matmul(ps[:, 6, 128:128 + FR], win[:, 0:DI], w2[:], start=True, stop=True).then_inc(set2, 1)
            pe.matmul(ps[0:FR, 7, 128 + DI:128 + 2 * DI], w2[:], win[:, DI:2 * DI], start=True, stop=True)
            pe.wait_ge(set2_sb, 1)
            pe.matmul(ps[0:FR, 7, 128:128 + DI], gx[:], cvt[:], start=True, stop=True).then_inc(set3, 1)
            pe.wait_ge(casts, 4)
            pe.wait_ge(onehot, 1)
            for i in range(CB):
                m = pe.matmul(ps[0:CB, 0, 0:B * NSK], indb[:, i * CB:(i + 1) * CB],
                              oh[:, i].rearrange("p b s -> p (b s)"), start=(i == 0), stop=(i == CB - 1))
            m.then_inc(tot_ready, 1)
            pe.wait_ge(onehot_r, 1)
            for i in range(CB):
                m = pe.matmul(ps[0:CB, 0, 256:256 + B * NSK], con("ind")[:, i * CB:(i + 1) * CB],
                              ohq[:, i].rearrange("p b s -> p (b s)"), start=(i == 0), stop=(i == CB - 1))
            m.then_inc(tot_ready, 1)
            pe.wait_ge(tot_sb, 2)
            for w, (t_in, m_in, data, totals) in enumerate(((trib[:], cmb, oh, tot), (con("tri"), cm, ohq, totr))):
                for i in range(CB):
                    dst = ps[:, 1 + i // 3, (i % 3) * B * NSK:(i % 3 + 1) * B * NSK]
                    if w == 1 and i % 3 == 0:
                        pe.wait_ge(cum_used, i // 3 + 1)
                    pe.matmul(dst, t_in, data[:, i].rearrange("p b s -> p (b s)"), start=True, stop=False)
                    m = pe.matmul(dst, m_in[:, i * 128:(i + 1) * 128], totals[:], start=False, stop=True)
                    if i % 3 == 2 or i == CB - 1:
                        m.then_inc(cum_ready, 1)
            pe.wait_ge(feat, 8)
            pe.transpose(ps[:, 0, 0:128], f2[:, 0, :], con("ident")).then_inc(ft_ready, 1)
            pe.wait_ge(ft_sb, 1)
            pe.wait_ge(bdc_ready, 1)
            for i in range(4):
                pe.matmul(ps[:, 1 + i, :], ftt[:], bdc[:, 8 * i:8 * i + 8, :].rearrange("p c e -> p (c e)"),
                          start=True, stop=True).then_inc(hc_ready, 1)
            pe.wait_ge(part_step, 5)
            psb = ps[:, 0, 0:384].bitcast(BF16).rearrange("p (i t) -> p i t", t=128)
            for i in range(3):
                for v in range(2):
                    m = pe.transpose(psb[:, 3 * v + i, :], parts[:, i, v, :], idb[:])
            m.then_inc(fts_ready, 1)
            pe.wait_ge(g_step, 4)
            pe.wait_ge(fts_sb, 1)
            pe.wait_ge(s_f36, 16 * 6)
            for w in range(2):
                wt = g36[:, 128 + w * DI:128 + (w + 1) * DI]
                if w == 0:
                    for i in range(4):
                        pe.matmul(ps[:, i, :], wt, f36[:, 1, i * HC:(i + 1) * HC], start=True, stop=True
                                  ).then_inc(xz_ready, 1)
                with pe.Fori(1 - w, B) as b:
                    for i in range(4):
                        pe.wait_ge(xz_done, w * Q + b * 4 + i - 3)
                        pe.matmul(ps[:, i, :], wt, f36[:, 1, ds(b * L + i * HC, HC)], start=True, stop=True
                                  ).then_inc(xz_ready, 1)

            def prep(s, u_ap, bc, dt):
                k = segment(s)[1]
                pe.matmul(bc, xb[:, k, :], u_ap, start=True, stop=True)
                pe.matmul(dt, wdt[:, k, :], u_ap, start=True, stop=True).then_inc(x_ready, 1)

            pe.wait_ge(xz_done, Q)
            for i in range(2):
                prep(0, u[:, i * HC:(i + 1) * HC], ps[0:BCR, 4 + 2 * i, :], ps[:, 5 + 2 * i, :])

            def spread(s, n, j, first):
                k = segment(s)[1]
                for h in range(2):
                    g = 2 * (s * N + n) + h
                    t = phys(k, h) * HC
                    opt_ge(pe, scan_done, g - 1, not (first and j == 0))
                    pe.matmul(ps[:, 2 + h, :], selb[0:BCR, ds(n, 1), :].rearrange("p o d -> p (o d)"),
                              pr[:, s % 2, t:t + HC], start=True, stop=True).then_inc(b_ready, 1)
                    opt_ge(pe, c_copied, g - 1, not (first and j == 0))
                    pe.matmul(ps[:, 4 + h, :], selb[0:BCR, ds(N + n, 1), :].rearrange("p o d -> p (o d)"),
                              pr[:, s % 2, t:t + HC], start=True, stop=True).then_inc(c_ready, 1)

            def add_up(s, n, j, start, stop=False):
                st = s * N + n
                pe.wait_ge(p_done, st + 1)
                for w in range(2):
                    m = pe.matmul(ps[:, w, :], con("ident"), pv[:, j, w * HC:(w + 1) * HC], start=start, stop=stop)
                m.then_inc(sum_done, 1)

            def turn(s, it, first):
                nx = s + 1
                for j in range(UN):
                    if j == 0 and nx < NSEG:
                        nb, nk, nc_ = segment(nx)
                        local = snapped(pe, it * SL if nk == 0 else it * -SL + (IT - 1) * SL)
                        pe.wait_ge(x_delta, prepared(nx, it))
                        prep(nx, u[:, ds(nb * L + nc_ * CH + local, SL)], ps[0:BCR, 6, 0:SL], ps[:, 6, SL:2 * SL])
                    spread(s, it * UN + j, j, first)
                    if isinstance(it, int):
                        if j >= 2:
                            if j == 2 and s > 0 and s % 4 != 2:
                                pe.wait_ge(y_taken, (0, 1, 0, 2)[s % 4] + 3 * (s // 4))
                            add_up(s, j - 2, j - 2, j == 2 and s % 4 != 2)
                        elif s > 0:
                            add_up(s - 1, N - 2 + j, 2 + j, False, j == 1 and (s - 1) % 4 != 1)
                    else:
                        add_up(s, it * UN + j - 2, (j + 2) % UN, False)

            pe.wait_ge(sel_ready, 1)
            for s in range(NSEG):
                pe.wait_ge(x_parts, prepared(s + 1, 0))
                opt_ge(pe, x_delta, 2, s == 0)
                turn(s, 0, s == 0)
                with pe.Fori(1, IT) as it:
                    turn(s, it, False)
            add_up(NSEG - 1, N - 2, 2, False)
            add_up(NSEG - 1, N - 1, 3, False, True)

            def last(qq, p):
                q = 2 * qq + p
                a, b_, c_, d = (4 * p + i for i in range(4))

                def s1():
                    pe.matmul(ps[:, a, :], con("cen128"), u[:, ds(q * HC, HC)], start=True, stop=True).then_inc(q_yc, 1)

                def s2():
                    pe.wait_ge(q_sq, q + 1)
                    if not isinstance(qq, int) or q >= 2:
                        pe.wait_ge(q_out, q - 1)
                    pe.matmul(ps[:, b_, :], con("one128"), sq[:, p, :], start=True, stop=True).then_inc(q_var, 1)

                def s3():
                    pe.wait_ge(q_t, q + 1)
                    pe.matmul(ps[:, c_, :], wou[:], tt[:, p, :], start=True, stop=False)
                    pe.matmul(ps[:, c_, :], g36[:, 0:128], f36[:, 0, ds(q * HC, HC)], start=False, stop=True
                              ).then_inc(q_o, 1)

                def s4():
                    pe.wait_ge(q_h1, q + 1)
                    pe.matmul(ps[:, d, :], con("cen64", E), h1[0:E, p, :], start=True, stop=True).then_inc(q_hc, 1)

                def s5():
                    pe.wait_ge(q_sq2, q + 1)
                    pe.matmul(ps[:, b_, :], con("one64", E), sq[0:E, p, :], start=True, stop=True).then_inc(q_var2, 1)

                def s6():
                    pe.wait_ge(q_hn, q + 1)
                    pe.matmul(ps[:, a, :], wi_[:], hn[0:E, p, :], start=True, stop=True).then_inc(q_w, 1)

                def layer(l, src, bank, ready, done):
                    def f():
                        pe.wait_ge(ready, q + 1)
                        if l == 0:
                            pe.wait_ge(we_loaded[p], 16 * GQ * (qq + 1))
                        pe.matmul(ps[:, bank, :], si[:, l, :], src[:, p, :], start=True, stop=False)
                        pe.matmul(ps[:, bank, :].rearrange("p (g t) -> p g t", t=TG), brp[:, l * HID:(l + 1) * HID],
                                  ohr[:, ds(q * GQ, GQ)].unsqueeze(2).to_broadcast([BR, GQ, TG]),
                                  start=False, stop=False)
                        for g in range(GQ):
                            m = pe.matmul(ps[:, bank, g * TG:(g + 1) * TG], we[:, p * GQ + g, l, :],
                                          src[:, p, g * TG:(g + 1) * TG], start=False, stop=(g == GQ - 1))
                        m.then_inc(done, 1)
                    return f

                def s9():
                    pe.wait_ge(q_f2, q + 1)
                    pe.matmul(ps[0:E, b_, :], wo_[:], fa[:, p, :], start=True, stop=True).then_inc(q_wo, 1)

                return (s1, s2, s3, s4, s5, s6, layer(0, fa, c_, q_f0, q_l0), layer(1, fb, d, q_f1, q_l1), s9)

            pe.wait_ge(y_taken, 6)
            pe.wait_ge(bias_step, 5)
            pe.wait_ge(si_ready, 1)
            both = [last(0, p) for p in range(2)]
            for st in zip(*both):
                for f in st:
                    f()
            with pe.Fori(1, Q // 2) as qq:
                both = [last(qq, p) for p in range(2)]
                for st in zip(*both):
                    for f in st:
                        f()


def constants():
    import numpy as np
    cf = np.zeros((128, CFW), np.float32)

    def put(name, a):
        cf[:a.shape[0], CF[name][0]:CF[name][0] + a.shape[1]] = a

    i = np.arange(128)
    eye = np.eye(128, dtype=np.float32)
    put("ident", eye)
    put("tri", (i[:, None] <= i[None, :]).astype(np.float32))
    put("cen128", eye - np.float32(1 / DI))
    put("one128", np.full((128, 128), 1 / DI, np.float32))
    pad = (np.arange(128) < E).astype(np.float32)
    put("cen64", (eye[:E] - np.float32(1 / E)) * pad)
    put("one64", np.full((E, 128), 1 / E, np.float32) * pad)
    put("iota", np.tile(np.arange(NSK, dtype=np.float32), (128, 1)))
    put("blk", (i[:, None] % NC == np.arange(NC)[None, :]).astype(np.float32))

    def part_masks(part):
        return np.stack([-1.0 * (part >= 1), -1.0 * (part >= 2)], 1).astype(np.float32)

    put("m36", part_masks(np.arange(FR) // 12))
    r = np.arange(BCR)
    put("mbc", part_masks((r % 64) // N))
    r = np.arange(3 * (NX + 1))
    put("m51", part_masks(r // (NX + 1)))
    e = r % (NX + 1)
    put("eid", np.stack([np.where(e < NX, e, -1e9), 1.0 * (e == NX)], 1).astype(np.float32))
    put("ind", np.tile(np.eye(CB, dtype=np.float32).reshape(1, -1), (128, 1)))
    sel = np.zeros((128, 2 * N), np.float32)
    for w in range(2):
        for n in range(N):
            for part in range(3):
                sel[64 * w + part * N + n, w * N + n] = 1.0
    put("sel", sel)
    cm = (np.arange(CB)[:, None, None] < np.arange(CB)[None, :, None]) * np.ones((1, 1, 128))
    return cf, cm.reshape(CB, CB * 128).astype(np.float32)


def kernel(**inputs):
    import numpy as np
    import concourse.bacc as _bacc
    from concourse.bass_utils import run_bass_kernel_spmd as _run

    x = {n: np.asarray(v) for n, v in inputs.items()}
    a = {n[8:]: v for n, v in x.items() if n.startswith("L0_attn_")}
    f = {n[7:]: v for n, v in x.items() if n.startswith("L0_ffn_")}
    t = {n[7:]: v for n, v in x.items() if n.startswith("L0_tok_")}
    f32 = np.float32

    def toks(v):
        return v.reshape(B, CB, 128).transpose(2, 0, 1).reshape(128, NC)

    def col(v):
        return np.concatenate([v, np.zeros(128 - v.shape[0], f32)])

    cf, cm = constants()
    m = np.zeros((E + 1, NF), f32)
    n0, n1 = t["skill_w"].shape[0], t["skill_w"].shape[0] + t["att_w"].shape[0]
    m[0:n0, 0], m[n0:n1, 1], m[n1:E, 2] = t["skill_w"], t["att_w"], t["mast_w"]
    m[0:n0, 3], m[n0:n1, 3], m[n1:E, 3] = t["skill_b"], t["att_b"], t["mast_b"]
    m[E, 3] = 1.0
    xp = a["x_proj_w"]
    xbc = np.zeros((DI, K, BCR), f32)
    for part in range(3):
        xbc[:, :, part * N:(part + 1) * N] = xp[:, R:R + N].transpose(2, 0, 1)
        xbc[:, :, 64 + part * N:64 + (part + 1) * N] = xp[:, R + N:R + 2 * N].transpose(2, 0, 1)
    wr = np.zeros((NX + 1, HID, NL, HID), f32)
    wr[:NX] = f["Wr"].transpose(1, 3, 0, 2)
    bb = np.concatenate([f["br"].transpose(1, 0, 2), f["bs"].transpose(1, 0, 2)], 0).reshape(NX + 1, NL * HID)
    route = f["route_id"].reshape(1, NR)
    arrays = {
        "tok": np.stack([toks(x["x"]), toks(x["mask_BS_i0_1"])], 1),
        "consts": cf, "cmask": cm,
        "chan": np.stack([a["conv_b"], a["dt_b"][0], a["dt_b"][1], a["Ds"][:DI], a["Ds"][DI:], a["ln_w"], a["ln_b"],
                          f["bi"], col(f["bo"])], 1),
        "tokm": np.concatenate([np.tile(m, (1, FR // NF)), np.repeat(m, NC, 1)], 1),
        "projt": np.pad(np.concatenate([t["proj_w"].T, t["proj_b"][None]], 0), ((0, 0), (0, 128 - E))),
        "wint": a["W_in"].T, "convt": a["conv_w"].T, "xbc": xbc,
        "xdt": xp[:, :R].transpose(1, 0, 2), "dtw": a["dt_w"].transpose(2, 0, 1),
        "alog": a["A_logs"].reshape(K, DI, N).transpose(1, 0, 2).reshape(DI, K * N),
        "wout": np.pad(a["W_out"].T, ((0, 0), (0, 128 - E))), "wit": f["Wi"].T, "ws": f["Ws"][:, 0].transpose(2, 0, 1), "wo": f["Wo"].T,
        "wr": wr, "brb": np.tile(bb, (3, 1)), "route": route, "routeb": np.tile(route, (3 * (NX + 1), 1)),
    }
    arrays = {n: np.ascontiguousarray(v) for n, v in arrays.items()}
    nc = _bacc.Bacc("TRN2", target_bir_lowering=False, num_devices=1)
    args = [nc.dram_tensor(n, v.shape, mybir.dt.from_np(v.dtype), kind="ExternalInput").ap()
            for n, v in arrays.items()]
    args.append(nc.dram_tensor("scratch", (2, 3, 128, 128), BF16, kind="Internal").ap())
    args.append(nc.dram_tensor("h_t", (E, T), F32, kind="ExternalOutput").ap())
    bass_lm_tower(nc, *args)
    r = _run(nc, [arrays], core_ids=[0])
    return np.ascontiguousarray(r.results[0]["h_t"].T).reshape(B, L, E)
```

```python
from contextlib import ExitStack

import concourse.bass as bass
from concourse import mybir

F32 = mybir.dt.float32
BF16 = mybir.dt.bfloat16
I32 = mybir.dt.int32
U16 = mybir.dt.uint16
ALU = mybir.AluOpType
ACT = mybir.ActivationFunctionType
AX = mybir.AxisListType
ds = bass.ds

B, L = 2, 2048
NSK = 75
E = 64
DI = 128
K = 2
N = 16
R = 16
HID = 128
NX = 16
NL = 2
NR = 64
TG = B * L // NR
T = B * L
NC = T // 128
CB = L // 128
CH = 1024
HC = 512
SL = 256
NSEG = B * K * (L // CH)
UN = 4
IT = N // UN
NF = 4
FR = 3 * 3 * NF
BR = 96
BCR = 112
EPS = 1e-5
BIG = 1e17
Q = T // HC
GQ = HC // TG

CF = {}
_at = 0
for _n, _w in (("ident", 128), ("tri", 128), ("cen128", 128), ("one128", 128), ("one64", 128),
               ("iota", NSK), ("m36", 2), ("mbc", 2), ("mbr", 2), ("eid", 2), ("indf", CB * CB), ("sel", 2 * N)):
    CF[_n] = (_at, _at + _w)
    _at += _w
CFW = _at
CBF = {"tri": (0, 128), "ind": (128, 128 + CB * CB), "ident": (128 + CB * CB, 256 + CB * CB)}
CBW = 256 + CB * CB
CHN = ["conv_b", "dt_b0", "dt_b1", "d0", "d1", "ln_w", "ln_b", "bi", "bo"]


def segment(s):
    b, r = divmod(s, 4)
    return b, (0, 0, 1, 1)[r], (0, 1, 1, 0)[r]


def bass_lm_tower(nc, tok, consts, constb, cmask, chan, tokm, projt, wint, convt, xbc, xdt, dtw, alog, wout, wit, ws, wo,
                  wr, brb, route, routeb, wsum, out):
    with ExitStack() as ctx:
        def sb(name, shape, dt=F32):
            return ctx.enter_context(nc.sbuf_tensor(name, shape, dt))

        def sem(name):
            return ctx.enter_context(nc.semaphore(name))

        ps = ctx.enter_context(nc.psum_tensor("ps", [128, 8, 512], F32))

        cf = sb("cf", [128, CFW])
        cbf = sb("cbf", [128, CBW], BF16)
        cm = sb("cm", [CB, CB * 128], BF16)
        ch = sb("ch", [128, len(CHN)])
        tm = sb("tm", [E + 1, FR])
        pt = sb("pt", [E + 1, 128])
        pmean = sb("pmean", [DI, 4])
        win = sb("win", [E, 2 * DI])
        cvt = sb("cvt", [DI, DI])
        xb = sb("xb", [DI, K, BCR])
        xd = sb("xd", [R, K, DI])
        dw = sb("dw", [R, K, DI])
        wdt = sb("wdt", [DI, K, DI])
        al = sb("al", [DI, K * N])
        na = sb("na", [DI, K * N])
        wou = sb("wou", [DI, 128])
        wi_ = sb("wi_", [128, HID])
        si = sb("si", [HID, NL, HID])
        wo_ = sb("wo_", [HID, 128])
        br = sb("br", [BR, NL * HID])
        brr = sb("brr", [BR, NL * HID])
        brh = sb("brh", [BR, NL * HID], BF16)
        brp = sb("brp", [BR, NL * HID], BF16)
        rtb = sb("rtb", [BR, NR], I32)
        ohr = sb("ohr", [BR, NR], BF16)
        rt = sb("rt", [1, NR], I32)
        rtw = sb("rtw", [1, 4, NR])
        slot = sb("slot", [1, NR], I32)
        selb = sb("selb", [128, 2 * N, 128], BF16)
        dsum = sb("dsum", [DI, 1])
        eps = sb("eps", [128, 1])
        ysv = sb("ysv", [DI, CH])

        tk = sb("tk", [128, 2, NC], I32)
        tf = sb("tf", [128, 2, NC])
        cmf = sb("cmf", [CB, CB * 128])
        tot = sb("tot", [CB, B * NSK], BF16)
        totr = sb("totr", [CB, B * NSK])
        f2 = sb("f2", [128, 2, NF * NC])
        ft = f2[:, 0, :].rearrange("p (f c) -> p f c", f=NF)
        ftn = f2[:, 1, :].rearrange("p (f c) -> p f c", f=NF)
        val = sb("val", [128, 3, NC])
        ss = sb("ss", [128, 3, NC])
        outer = sb("outer", [128, NF * NF, NC])
        outg = sb("outg", [128, NF * NF, NC])
        gram = sb("gram", [128, NF * NF])
        wpair = sb("wpair", [E, NF, NF])
        parts = sb("parts", [128, 2, NC, 3, 3, NF], BF16)
        rest = sb("rest", [128, 2, NF * NC])
        w2 = sb("w2", [E, FR])
        gx = sb("gx", [DI, FR])
        GC = 3 * 128
        gwr = sb("gwr", [FR, GC])
        gwh = sb("gwh", [FR, 2, GC], BF16)
        g36 = sb("g36", [FR, GC], BF16)
        f36 = sb("f36", [FR, 2, T], BF16)

        u = sb("u", [DI, T])
        z = sb("z", [DI, T])
        wall = z[:].rearrange("p (x l j) -> p x l j", x=NX, l=NL)
        dcen = sb("dcen", [DI, DI])
        dl = sb("dl", [DI, 2, CH])
        du = sb("du", [DI, 2, CH])
        pr = sb("pr", [BCR, 2, CH], BF16)
        xe = sb("xe", [DI, CH])
        xl = sb("xl", [DI, CH])
        xh = sb("xh", [BCR, CH], BF16)
        xr = sb("xr", [BCR, CH])
        xm = sb("xm", [BCR, CH], BF16)
        carry = sb("carry", [DI, N])
        big = sb("big", [128, 5 * UN // 2 * CH + 512])
        oh = big[:, 0:1200].bitcast(BF16).rearrange("p (c b s) -> p c b s", c=CB, b=B)
        ohq = big[:, 1200:3600].rearrange("p (c b s) -> p c b s", c=CB, b=B)
        prod = big[:, 3600:8400].rearrange("p (w c b s) -> p w c b s", w=2, c=CB, b=B)
        bv = big[:, 0:UN * CH].rearrange("p (r t) -> p r t", r=UN)
        pv = big[:, UN * CH:2 * UN * CH].rearrange("p (r t) -> p r t", r=UN)
        hv = big[:, 2 * UN * CH:2 * UN * CH + 2 * CH].rearrange("p (r t) -> p r t", r=2)
        sq, rs, tt, hn, fa, fb, h1, ot = (big[:, 2 * HC * w:2 * HC * (w + 1)].rearrange("p (r t) -> p r t", r=2)
                                          for w in range(8))
        wes = sb("wes", [HID, 2 * GQ * NL * HID])
        we = wes[:].rearrange("p (r l j) -> p r l j", r=2 * GQ, l=NL)

        s_tok, s_con, s_cm, s_w, s_late = (sem(n) for n in (
            "tok_loaded", "consts_loaded", "cmask_loaded", "weights_loaded", "late_loaded"))
        s_cb, s_si, s_wall, wall_summed, wsum_stored = (sem(n) for n in (
            "constb_loaded", "shared_loaded", "experts_in", "experts_summed", "experts_stored"))
        cmf_ready, sel_ready, neg_a, exp_a = sem("cmf_ready"), sem("sel_ready"), sem("neg_a"), sem("exp_a")
        proj_c, set1, set1_sb, set2, set2_sb, set3 = (sem(n) for n in (
            "proj_centred", "setup1", "setup1_copied", "setup2", "setup2_copied", "setup3"))
        g_step, bias_step, route_step, dsum_ready, dcen_ready, si_ready = (sem(n) for n in (
            "g_step", "bias_step", "route_step", "dsum_ready", "dcen_ready", "si_ready"))
        pair_ready, gram_ready, gram_sb, wou_step = (sem(n) for n in (
            "pair_ready", "gram_ready", "gram_copied", "wou_step"))
        tok_f, onehot, onehot_r, tot_ready, tot_sb, cum_ready, cum_used = (sem(n) for n in (
            "tok_float", "onehot", "onehot_r", "totals", "totals_copied", "cum_ready", "cum_used"))
        feat, ss_ready, rstd_ready = (sem(n) for n in ("features", "ss_ready", "rstd_ready"))
        ss_step, eps_set = sem("ss_step"), sem("eps_set")
        part_step, fts_ready, fts_act, fts_dve = (sem(n) for n in (
            "part_step", "parts_t", "parts_t_by_act", "parts_t_by_dve"))
        xz_ready, xz_done = sem("xz_ready"), sem("xz_done")
        x_ready, x_exp, x_hi, x_min, x_rest, x_ln, x_mid, x_parts, x_delta, x_du = (sem(n) for n in (
            "x_ready", "x_exp", "x_hi", "x_min", "x_rest", "x_ln", "x_mid", "x_parts", "x_delta", "x_du"))
        b_ready, b_copied, c_ready, a_ready, mul_done, scan_done = (sem(n) for n in (
            "b_ready", "b_copied", "c_ready", "a_ready", "mul_done", "scan_done"))
        carry_saved, p_done, sum_done, y_taken = (sem(n) for n in (
            "carry_saved", "p_done", "sum_done", "y_taken"))
        q_sq, q_var, q_ln, q_rs, q_t1, q_t, q_o, q_h1 = (sem(n) for n in (
            "y_squared", "y_var", "y_ln", "y_rstd", "y_scaled", "y_gated", "o_ready", "h1_ready"))
        q_sq2, q_var2, q_ln2, q_rs2, q_hn, q_w, q_f0, q_l0, q_f1, q_l1, q_f2, q_wo, q_out = (
            sem(n) for n in ("h1_squared", "h1_var", "h1_ln", "h1_rstd", "h1_normed", "wi_ready", "f0_ready",
                             "l0_ready", "f1_ready", "l1_ready", "f2_ready", "wo_ready", "out_ready"))
        we_loaded = [sem(f"experts_loaded{p}") for p in range(2)]
        out_stored = [sem(f"out_stored{p}") for p in range(2)]

        def con(name, rows=128):
            a, b_ = CF[name]
            return cf[0:rows, a:b_]

        def chn(name, rows=128):
            i = CHN.index(name)
            return ch[0:rows, i:i + 1]

        def cb_view(ap):
            return ap.rearrange("p (b c) -> p c b", b=B)

        def prepared(s, it):
            return it if s == 0 else 2 + (s - 1) * IT + it

        def slice_at(s, it):
            b, k, c = segment(s)
            return b * L + c * CH + (it * SL if k == 0 else it * -SL + (IT - 1) * SL)

        def phys(k, h):
            return h if k == 0 else 1 - h

        def cbn(name, rows=128):
            a, b_ = CBF[name]
            return cbf[0:rows, a:b_]

        def is_first(it):
            return isinstance(it, int)

        def opt_ge(eng, s, v, ok):
            if ok:
                eng.wait_ge(s, v)

        def snapped(eng, v):
            return v if isinstance(v, int) else eng.snap(v)

        def prep_parts(eng, s, it, width, o, local):
            eng.wait_ge(x_mid, prepared(s, it) + 1)
            eng.tensor_tensor(pr[:, s % 2, ds(local, width)], xm[:, o:o + width], xr[:, o:o + width], ALU.add
                              ).then_inc(x_parts, 1)

        def prep_du(eng, s, it, width, local, t0):
            eng.wait_ge(x_delta, prepared(s, it) + 1)
            eng.tensor_tensor(du[:, s % 2, ds(local, width)], dl[:, s % 2, ds(local, width)], u[:, ds(t0, width)],
                              ALU.mult).then_inc(x_du, 1)

        block = ctx.enter_context(nc.Block())

        @block.sync
        def _(sp):
            sp.dma_start(tk[:], tok).then_inc(s_tok, 16)
            sp.dma_start(cf[:], consts).then_inc(s_con, 16)
            sp.dma_start(cbf[:], constb.bitcast(BF16)).then_inc(s_cb, 16)
            sp.dma_start(cm[:], cmask.bitcast(BF16)).then_inc(s_cm, 16)
            sp.dma_start(si[:], ws).then_inc(s_si, 16)
            sp.dma_start(wall, wr.rearrange("x i l j -> i x l j")).then_inc(s_wall, 16)
            for dst, src in ((al, alog), (wou, wout), (wi_, wit), (wo_, wo), (br, brb), (rtb, routeb), (rt, route)):
                sp.dma_start(dst[:], src).then_inc(s_late, 16)
            sp.wait_ge(si_ready, 1)
            sp.wait_ge(wall_summed, 1)
            sp.dma_start(wsum[0:NX].rearrange("x i l j -> i x l j"), wall).then_inc(wsum_stored, 16)
            sp.dma_start(wsum[NX], si[:]).then_inc(wsum_stored, 16)

            def experts(q):
                for g in range(GQ):
                    e = sp.value_load(slot[0:1, ds(q * GQ + g, 1)], min_val=0, max_val=NX)
                    sp.dma_start(we[:, g, :, :], wsum[ds(e, 1)].rearrange("o i l j -> i (o l) j")
                                 ).then_inc(we_loaded[0], 16)

            sp.wait_ge(route_step, 5)
            sp.wait_ge(wsum_stored, 32)
            experts(0)
            with sp.Fori(0, Q // 2 - 1) as qq:
                sp.wait_ge(q_l1, 2 * qq + 1)
                experts(2 * qq + 2)
                for p in range(2):
                    sp.wait_ge(q_out, 2 * qq + p + 1)
                    sp.dma_start(out[:, ds((2 * qq + p) * HC, HC)], ot[0:E, p, :]).then_inc(out_stored[p], 16)
            for q in (Q - 2, Q - 1):
                sp.wait_ge(q_out, q + 1)
                sp.dma_start(out[:, q * HC:(q + 1) * HC], ot[0:E, q % 2, :]).then_inc(out_stored[q % 2], 16)
            for p in range(2):
                sp.wait_ge(out_stored[p], 16 * Q // 2)

        @block.gpsimd
        def _(pool):
            pool.wait_ge(s_cm, 16)
            pool.tensor_copy(cmf[:], cm[:]).then_inc(cmf_ready, 1)
            pool.wait_ge(s_con, 16)
            pool.wait_ge(si_ready, 1)
            pool.wait_ge(s_wall, 16)
            pool.tensor_tensor(wall, wall, si[:].unsqueeze(1).to_broadcast([HID, NX, NL, HID]), ALU.add
                               ).then_inc(wall_summed, 1)
            pool.tensor_copy(selb[:], con("sel").unsqueeze(2).to_broadcast([128, 2 * N, 128])).then_inc(sel_ready, 1)
            pool.wait_ge(route_step, 5)
            pool.wait_ge(wsum_stored, 32)

            def experts(q):
                for g in range(GQ):
                    e = pool.value_load(slot[0:1, ds(q * GQ + g, 1)], min_val=0, max_val=NX)
                    pool.dma_start(we[:, GQ + g, :, :], wsum[ds(e, 1)].rearrange("o i l j -> i (o l) j")
                                   ).then_inc(we_loaded[1], 16)

            experts(1)

            def product(s, it, j):
                st = s * N + it * UN + j
                pool.wait_ge(b_copied, 2 * st + 2)
                pool.tensor_tensor(bv[:, j, :], bv[:, j, :], du[:, s % 2, :], ALU.mult).then_inc(mul_done, 1)

            def turn(s, it):
                nx = s + 1
                if nx < NSEG:
                    nb, nk, nc_ = segment(nx)
                    local = snapped(pool, it * SL if nk == 0 else it * -SL + (IT - 1) * SL)
                for j in range(UN):
                    product(s, it, j)
                    if j == 1 and nx < NSEG:
                        prep_parts(pool, nx, it, SL, 0, local)
                    if j == 2 and nx < NSEG:
                        prep_du(pool, nx, it, SL, local, nb * L + nc_ * CH + local)

            for s in range(NSEG):
                pool.wait_ge(x_du, prepared(s + 1, 0))
                turn(s, 0)
                with pool.Fori(1, IT) as it:
                    turn(s, it)
            with pool.Fori(0, Q // 2 - 1) as qq:
                pool.wait_ge(q_l1, 2 * qq + 2)
                experts(2 * qq + 3)

        @block.scalar
        def _(act):
            for dst, src in ((tm, tokm), (pt, projt), (win, wint), (cvt, convt), (xb, xbc), (xd, xdt), (dw, dtw),
                             (ch, chan)):
                act.dma_start(dst[:], src).then_inc(s_w, 16)
            act.preload_act_table_set("natural_log_exp_and_others")
            act.wait_ge(set1, 1)
            act.activation(w2[:], ps[0:E, 7, 0:FR], ACT.Copy).then_inc(set1_sb, 1)
            act.activation(wdt[:], ps[:, 6, 256:512].rearrange("p (k d) -> p k d", k=K), ACT.Copy).then_inc(set1_sb, 1)
            act.wait_ge(set2, 1)
            act.activation(gx[:], ps[:, 5, 0:FR], ACT.Copy).then_inc(set2_sb, 1)
            act.wait_ge(gram_ready, 1)
            act.activation(gram[:], ps[:, 4, 0:NF * NF], ACT.Copy).then_inc(gram_sb, 1)
            act.wait_ge(s_late, 16 * 7)
            act.activation(na[:], al[:], ACT.Exp).then_inc(exp_a, 1)
            act.wait_ge(exp_a, 1)
            act.activation(na[:], na[:], ACT.Copy, scale=-1.0).then_inc(neg_a, 1)
            act.wait_ge(tot_ready, 2)
            act.activation(tot[:], ps[0:CB, 0, 0:B * NSK], ACT.Copy).then_inc(tot_sb, 1)
            act.activation(totr[:], ps[0:CB, 0, 256:256 + B * NSK], ACT.Copy).then_inc(tot_sb, 1)
            act.wait_ge(ss_ready, 4)
            act.activation(ss[:, 2, :], ss[:, 1, :], ACT.Ln).then_inc(rstd_ready, 1)
            act.wait_ge(rstd_ready, 1)
            act.activation(ss[:, 0, :], ss[:, 2, :], ACT.Exp, scale=-0.5).then_inc(rstd_ready, 1)
            for i in range(2):
                act.wait_ge(fts_ready, i + 1)
                act.activation(f36[:, 1, i * 1024:(i + 1) * 1024], ps[0:FR, i, :].bitcast(BF16), ACT.Copy
                               ).then_inc(fts_act, 1)
            for w, (dst, bias) in enumerate(((u, chn("conv_b")), (z, 0.0))):
                if w == 1:
                    act.wait_ge(wsum_stored, 32)
                with act.Fori(0, B) as b:
                    for i in range(4):
                        act.wait_ge(xz_ready, w * Q + b * 4 + i + 1)
                        act.activation(dst[:, ds(b * L + i * HC, HC)], ps[:, 4 + i, :], ACT.Silu, bias=bias
                                       ).then_inc(xz_done, 1)
            act.preload_act_table_set("natural_log_exp_and_others")

            def prep_exp(s, it, t0, width, bank, bc, o):
                _, k, _ = segment(s)
                act.wait_ge(x_ready, prepared(s, it) + 1)
                act.activation(xe[:, o:o + width], bank[:, :], ACT.Exp, bias=chn(f"dt_b{k}")).then_inc(x_exp, 1)
                act.activation(xh[:, o:o + width], bc, ACT.Identity, scale=con("mbc", BCR)[:, 0:1]).then_inc(x_hi, 1)

            def prep_ln(s, it, width, o):
                act.wait_ge(x_min, prepared(s, it) + 1)
                act.activation(xl[:, o:o + width], xe[:, o:o + width], ACT.Ln, bias=1.0).then_inc(x_ln, 1)
                act.wait_ge(x_rest, prepared(s, it) + 1)
                act.activation(xm[:, o:o + width], xr[:, o:o + width], ACT.Identity, scale=con("mbc", BCR)[:, 1:2]
                               ).then_inc(x_mid, 1)

            for i in range(2):
                prep_exp(0, i, i * HC, HC, ps[:, 1 + 2 * i, :], ps[0:BCR, 2 * i, :], i * HC)
            for i in range(2):
                prep_ln(0, i, HC, i * HC)

            def copy_b(s, n, j, h):
                s, n = (s + 1, n - N) if is_first(n) and n >= N else (s, n)
                g = 2 * (s * N + n) + h
                t = phys(segment(s)[1], h) * HC
                act.wait_ge(b_ready, g + 1)
                act.activation(bv[:, j, t:t + HC], ps[:, 7, :], ACT.Copy).then_inc(b_copied, 1)

            def state(s, n, j, ahead):
                _, k, _ = segment(s)
                for h in range(2):
                    g = 2 * (s * N + n) + h
                    t = phys(k, h) * HC
                    opt_ge(act, scan_done, g - 1, not (s == 0 and is_first(n) and n == 0))
                    if ahead:
                        copy_b(s, n + 2, (j + 2) % UN, h)
                    act.activation(ps[:, 2 + h, :], dl[:, s % 2, t:t + HC], ACT.Exp,
                                   scale=na[:, ds(k * N + n, 1)]).then_inc(a_ready, 1)

            def take_y(s):
                b, k, c = segment(s)
                act.wait_ge(sum_done, N * (s + 1))
                act.activation(ysv[:] if s % 4 == 0 else u[:, b * L + c * CH:b * L + (c + 1) * CH],
                               ps[:, 0:2, :].rearrange("p w t -> p (w t)"), ACT.Copy).then_inc(y_taken, 1)

            def turn(s, it):
                for j in range(UN):
                    if j == 0 and s + 1 < NSEG:
                        prep_exp(s + 1, it, None, SL, ps[:, 6, SL:2 * SL], ps[0:BCR, 6, 0:SL], 0)
                    state(s, it * UN + j, j, not (s == NSEG - 1 and is_first(it) and it == IT - 1 and j >= 2))
                    if j == 0 and s + 1 < NSEG:
                        prep_ln(s + 1, it, SL, 0)
                    if is_first(it) and it == 0 and j == 2 and s > 0 and (s - 1) % 4 != 1:
                        take_y(s - 1)

            act.wait_ge(neg_a, 1)
            act.wait_ge(x_delta, 2)
            for n in range(2):
                for h in range(2):
                    copy_b(0, n, n, h)
            for s in range(NSEG):
                act.wait_ge(x_delta, prepared(s + 1, 0))
                turn(s, 0)
                with act.Fori(1, IT - 1) as it:
                    turn(s, it)
                turn(s, IT - 1)
            take_y(NSEG - 1)

            def last(q, p):
                a, b_, c_, d = (4 * p + i for i in range(4))

                def s1():
                    act.activation(sq[:, p, :], u[:, ds(q * HC, HC)], ACT.Square).then_inc(q_sq, 1)

                def s2():
                    act.wait_ge(q_var, q + 1)
                    act.activation(rs[:, p, :], ps[:, b_, :], ACT.Ln, bias=eps[:, 0:1]).then_inc(q_ln, 1)

                def s3():
                    act.wait_ge(q_ln, q + 1)
                    act.activation(rs[:, p, :], rs[:, p, :], ACT.Exp, scale=-0.5).then_inc(q_rs, 1)

                def s4():
                    act.wait_ge(q_o, q + 1)
                    act.activation(h1[0:E, p, :], ps[0:E, c_, :], ACT.Copy).then_inc(q_h1, 1)

                def s5():
                    act.wait_ge(q_o, q + 1)
                    act.activation(sq[E:128, p, :], ps[E:128, c_, :], ACT.Square).then_inc(q_sq2, 1)

                def s6():
                    act.wait_ge(q_var2, q + 1)
                    act.activation(rs[E:128, p, :], ps[E:128, b_, :], ACT.Ln, bias=eps[E:128, 0:1]).then_inc(q_ln2, 1)

                def s7():
                    act.wait_ge(q_ln2, q + 1)
                    act.activation(rs[E:128, p, :], rs[E:128, p, :], ACT.Exp, scale=-0.5).then_inc(q_rs2, 1)

                def s8():
                    act.wait_ge(q_w, q + 1)
                    act.activation(fa[:, p, :], ps[:, a, :], ACT.Relu, bias=chn("bi")).then_inc(q_f0, 1)

                def s9():
                    act.wait_ge(q_l0, q + 1)
                    act.activation(fb[:, p, :], ps[:, c_, :], ACT.Relu).then_inc(q_f1, 1)

                def s10():
                    act.wait_ge(q_l1, q + 1)
                    act.activation(fa[:, p, :], ps[:, d, :], ACT.Relu).then_inc(q_f2, 1)

                return (s1, s2, s3, s5, s4, s6, s7, s8, s9, s10)

            act.wait_ge(y_taken, 6)
            with act.Fori(0, Q // 2) as qq:
                both = [last(2 * qq + p, p) for p in range(2)]
                for st in zip(*both):
                    for f in st:
                        f()

        @block.vector
        def _(dve):
            dve.memset(eps[:], EPS).then_inc(eps_set, 1)
            dve.wait_ge(s_tok, 16)
            dve.tensor_copy(tf[:], tk[:]).then_inc(tok_f, 1)
            dve.wait_ge(s_con, 16)
            dve.wait_ge(tok_f, 1)
            iot = con("iota").unsqueeze(1).unsqueeze(1).to_broadcast([128, CB, B, NSK])
            qv = cb_view(tf[:, 0, :]).unsqueeze(3).to_broadcast([128, CB, B, NSK])
            rv = cb_view(tf[:, 1, :]).unsqueeze(3).to_broadcast([128, CB, B, NSK])
            dve.tensor_tensor(oh, iot, qv, ALU.is_equal).then_inc(onehot, 1)
            dve.wait_ge(onehot, 1)
            dve.tensor_tensor(ohq, oh, rv, ALU.mult).then_inc(onehot_r, 1)
            dve.wait_ge(s_si, 16)
            dve.tensor_tensor(si[:], si[:], con("ident").unsqueeze(1).to_broadcast([HID, NL, HID]), ALU.add
                              ).then_inc(si_ready, 1)
            dve.wait_ge(s_w, 16 * 8)
            dve.tensor_reduce(pmean[0:E + 1, 0:1], pt[:, 0:E], AX.X, ALU.add).then_inc(proj_c, 1)
            dve.wait_ge(proj_c, 1)
            dve.tensor_scalar(pmean[0:E + 1, 1:2], pmean[0:E + 1, 0:1], -1.0 / E, None, ALU.mult).then_inc(proj_c, 1)
            dve.wait_ge(proj_c, 2)
            dve.tensor_scalar(pt[:, E:2 * E], pt[:, 0:E], pmean[0:E + 1, 1:2], None, ALU.add).then_inc(proj_c, 1)
            dve.tensor_scalar(val[:, 0, :], tf[:, 0, :], 0.0, None, ALU.is_ge).then_inc(feat, 1)
            dve.wait_ge(feat, 1)
            dve.scalar_tensor_tensor(ft[:, 3, :], tf[:, 0, :], float(NSK), val[:, 0, :], ALU.is_lt, ALU.mult
                                     ).then_inc(feat, 1)
            dve.wait_ge(feat, 2)
            dve.tensor_tensor(ft[:, 0, :], tf[:, 0, :], ft[:, 3, :], ALU.mult).then_inc(feat, 1)
            dve.wait_ge(set1_sb, 1)
            dve.tensor_tensor(wpair[:], w2[:, 0:NF].unsqueeze(2).to_broadcast([E, NF, NF]),
                              w2[:, 0:NF].unsqueeze(1).to_broadcast([E, NF, NF]), ALU.mult).then_inc(pair_ready, 1)
            gp = ps[0:FR, 7, 0:GC]
            dve.wait_ge(set3, 1)
            dve.tensor_copy(gwh[:, 0, :], gp).then_inc(g_step, 1)
            dve.wait_ge(g_step, 1)
            dve.scalar_tensor_tensor(gwr[:], gwh[:, 0, :], con("m36", FR)[:, 0:1], gp, ALU.mult, ALU.add
                                     ).then_inc(g_step, 1)
            dve.wait_ge(g_step, 2)
            dve.tensor_copy(gwh[:, 1, :], gwr[:]).then_inc(g_step, 1)
            dve.wait_ge(g_step, 3)
            dve.scalar_tensor_tensor(g36[:], gwh[:, 1, :], con("m36", FR)[:, 1:2], gwr[:], ALU.mult, ALU.add
                                     ).then_inc(g_step, 1)
            for w in range(2):
                for i in range(6):
                    n = min(3, CB - 3 * i)
                    dve.wait_ge(cum_ready, 6 * w + i + 1)
                    dve.tensor_tensor(prod[:, w, 3 * i:3 * i + n].rearrange("p c b s -> p (c b s)"),
                                      ps[:, 1 + i, 0:n * B * NSK],
                                      oh[:, 3 * i:3 * i + n].rearrange("p c b s -> p (c b s)"), ALU.mult
                                      ).then_inc(cum_used, 1)
                if w == 0:
                    dve.wait_ge(cum_used, 6)
                    dve.tensor_reduce(cb_view(ft[:, 1, :]), prod[:, 0], AX.X, ALU.add).then_inc(feat, 1)
                    dve.wait_ge(feat, 4)
                    dve.tensor_scalar(val[:, 0, :], ft[:, 1, :], 1.0, None, ALU.max).then_inc(feat, 1)
                    dve.wait_ge(feat, 5)
                    dve.reciprocal(val[:, 1, :], val[:, 0, :]).then_inc(feat, 1)
            dve.wait_ge(cum_used, 12)
            dve.tensor_reduce(cb_view(val[:, 2, :]), prod[:, 1], AX.X, ALU.add).then_inc(feat, 1)
            dve.wait_ge(feat, 7)
            dve.tensor_tensor(ft[:, 2, :], val[:, 2, :], val[:, 1, :], ALU.mult).then_inc(feat, 1)
            dve.wait_ge(feat, 8)
            dve.tensor_tensor(outer[:].rearrange("p (f g) c -> p f g c", f=NF),
                              ft.unsqueeze(2).to_broadcast([128, NF, NF, NC]),
                              ft.unsqueeze(1).to_broadcast([128, NF, NF, NC]), ALU.mult).then_inc(ss_ready, 1)
            dve.wait_ge(ss_ready, 1)
            dve.wait_ge(gram_sb, 1)
            dve.tensor_tensor(outg[:], outer[:], gram[:].unsqueeze(2).to_broadcast([128, NF * NF, NC]), ALU.mult
                              ).then_inc(ss_ready, 1)
            dve.wait_ge(ss_ready, 2)
            dve.tensor_reduce(ss[:, 0, :], outg[:].rearrange("p f c -> p c f"), AX.X, ALU.add).then_inc(ss_ready, 1)
            dve.wait_ge(ss_ready, 3)
            dve.tensor_scalar(ss[:, 1, :], ss[:, 0, :], 0.0, EPS, ALU.max, ALU.add).then_inc(ss_ready, 1)

            def in_parts(v, t0):
                fv = f2[:, v, :].rearrange("p (f c) -> p c f", f=NF)
                rv = rest[:, v, :].rearrange("p (f c) -> p c f", f=NF)

                def thrice(ap):
                    return ap.unsqueeze(2).to_broadcast([128, NC, 3, NF])

                dve.tensor_copy(parts[:, v, :, 0], thrice(fv)).then_inc(part_step, 1)
                dve.wait_ge(part_step, t0 + 1)
                dve.tensor_tensor(rv, fv, parts[:, v, :, 0, 0], ALU.subtract).then_inc(part_step, 1)
                dve.wait_ge(part_step, t0 + 2)
                dve.tensor_copy(parts[:, v, :, 1], thrice(rv)).then_inc(part_step, 1)
                dve.wait_ge(part_step, t0 + 3)
                dve.tensor_tensor(parts[:, v, :, 2], thrice(rv), parts[:, v, :, 1], ALU.subtract
                                  ).then_inc(part_step, 1)

            in_parts(0, 0)
            dve.wait_ge(rstd_ready, 2)
            dve.tensor_tensor(ftn, ft, ss[:, 0, :].unsqueeze(1).to_broadcast([128, NF, NC]), ALU.mult
                              ).then_inc(part_step, 1)
            dve.wait_ge(part_step, 5)
            in_parts(1, 5)
            for i in range(6):
                dve.wait_ge(fts_ready, i + 3)
                v, c0 = (1, 2 + i) if i < 2 else (0, i - 2)
                dve.tensor_copy(f36[:, v, c0 * 1024:(c0 + 1) * 1024], ps[0:FR, c0, :].bitcast(BF16)
                                ).then_inc(fts_dve, 1)
            dve.wait_ge(s_late, 16 * 7)
            dve.tensor_tensor(dsum[:], chn("d0"), chn("d1"), ALU.add).then_inc(dsum_ready, 1)
            dve.wait_ge(dsum_ready, 1)
            dve.tensor_scalar(dcen[:], con("cen128"), dsum[:, 0:1], None, ALU.mult).then_inc(dcen_ready, 1)
            dve.tensor_reduce(pmean[:, 2:3], wou[:, 0:E], AX.X, ALU.add).then_inc(wou_step, 1)
            dve.wait_ge(wou_step, 1)
            dve.tensor_scalar(pmean[:, 3:4], pmean[:, 2:3], -1.0 / E, None, ALU.mult).then_inc(wou_step, 1)
            dve.wait_ge(wou_step, 2)
            dve.tensor_scalar(wou[:, E:2 * E], wou[:, 0:E], pmean[:, 3:4], None, ALU.add).then_inc(wou_step, 1)
            dve.tensor_copy(brh[:], br[:]).then_inc(bias_step, 1)
            dve.wait_ge(bias_step, 1)
            dve.scalar_tensor_tensor(brr[:], brh[:], con("mbr", BR)[:, 0:1], br[:], ALU.mult, ALU.add
                                     ).then_inc(bias_step, 1)
            dve.wait_ge(bias_step, 2)
            dve.tensor_copy(brh[:], brr[:]).then_inc(bias_step, 1)
            dve.wait_ge(bias_step, 3)
            dve.scalar_tensor_tensor(brp[:], brh[:], con("mbr", BR)[:, 1:2], brr[:], ALU.mult, ALU.add
                                     ).then_inc(bias_step, 1)
            dve.tensor_scalar(ohr[:], rtb[:], con("eid", BR)[:, 0:1], con("eid", BR)[:, 1:2], ALU.is_equal, ALU.max
                              ).then_inc(bias_step, 1)
            dve.tensor_copy(rtw[:, 0, :], rt[:]).then_inc(route_step, 1)
            dve.wait_ge(route_step, 1)
            dve.tensor_scalar(rtw[:, 1, :], rtw[:, 0, :], 0.0, None, ALU.is_ge).then_inc(route_step, 1)
            dve.wait_ge(route_step, 2)
            dve.scalar_tensor_tensor(rtw[:, 2, :], rtw[:, 0, :], float(NX), rtw[:, 1, :], ALU.is_lt, ALU.mult
                                     ).then_inc(route_step, 1)
            dve.wait_ge(route_step, 3)
            dve.scalar_tensor_tensor(rtw[:, 3, :], rtw[:, 0, :], -float(NX), rtw[:, 2, :], ALU.add, ALU.mult
                                     ).then_inc(route_step, 1)
            dve.wait_ge(route_step, 4)
            dve.tensor_scalar(slot[:], rtw[:, 3, :], float(NX), None, ALU.add).then_inc(route_step, 1)

            def prep_a(s, it, width, bc, o):
                t = prepared(s, it)
                dve.wait_ge(x_exp, t + 1)
                dve.tensor_scalar(xe[:, o:o + width], xe[:, o:o + width], BIG, None, ALU.min).then_inc(x_min, 1)
                dve.wait_ge(x_hi, t + 1)
                dve.tensor_tensor(xr[:, o:o + width], xh[:, o:o + width], bc, ALU.add).then_inc(x_rest, 1)

            def prep_b(s, it, width, bank, o, dst):
                k = segment(s)[1]
                dve.wait_ge(x_ln, prepared(s, it) + 1)
                dve.scalar_tensor_tensor(dst, bank, chn(f"dt_b{k}"), xl[:, o:o + width], ALU.add, ALU.max
                                         ).then_inc(x_delta, 1)

            for i in range(2):
                prep_a(0, i, HC, ps[0:BCR, 2 * i, :], i * HC)
            for i in range(2):
                prep_b(0, i, HC, ps[:, 1 + 2 * i, :], i * HC, dl[:, 0, i * HC:(i + 1) * HC])
                prep_parts(dve, 0, i, HC, i * HC, i * HC)
                prep_du(dve, 0, i, HC, i * HC, i * HC)

            def product(s, n, j, h, first):
                st = s * N + n
                g = 2 * st + h
                t = phys(segment(s)[1], h) * HC
                dve.wait_ge(scan_done, g + 1)
                dve.wait_ge(c_ready, g + 1)
                if h == 0:
                    opt_ge(dve, sum_done, st - UN + 1, not first)
                dve.tensor_tensor(pv[:, j, t:t + HC], ps[:, 4 + h, :], hv[:, j % 2, t:t + HC], ALU.mult
                                  ).then_inc(p_done, 1)

            def state(s, n, j):
                b, k, c = segment(s)
                start = s % 2 == 0
                st = s * N + n
                first = s == 0 and is_first(n) and n < UN

                def way(ap):
                    return ap if k == 0 else ap[:, ::-1]

                for h in range(2):
                    g = 2 * st + h
                    t = phys(k, h) * HC
                    if h == 0:
                        opt_ge(dve, p_done, 2 * st - 2, not (s == 0 and is_first(n) and n < 2))
                        dve.wait_ge(mul_done, st + 1)
                        initial = 0.0 if start else carry[:, ds(n, 1)]
                    else:
                        e = phys(k, 0) * HC + (HC - 1 if k == 0 else 0)
                        initial = hv[:, j % 2, e:e + 1]
                        dve.wait_ge(scan_done, g)
                    dve.wait_ge(a_ready, g + 1)
                    dve.tensor_tensor_scan(way(hv[:, j % 2, t:t + HC]), way(ps[:, 2 + h, :]),
                                           way(bv[:, j, t:t + HC]), initial, ALU.mult, ALU.add).then_inc(scan_done, 1)
                    if h == 1:
                        product(s, n, j, 0, first)
                    elif is_first(n) and n == 0:
                        if s > 0:
                            product(s - 1, N - 1, UN - 1, 1, False)
                    else:
                        product(s, n - 1, (j - 1) % UN, 1, first)
                if start:
                    e = CH - 1 if k == 0 else 0
                    dve.wait_ge(scan_done, 2 * st + 2)
                    dve.tensor_copy(carry[:, ds(n, 1)], hv[:, j % 2, e:e + 1]).then_inc(carry_saved, 1)

            def turn(s, it):
                nx = s + 1
                if nx < NSEG:
                    nk = segment(nx)[1]
                    local = snapped(dve, it * SL if nk == 0 else it * -SL + (IT - 1) * SL)
                for j in range(UN):
                    if j == 0 and nx < NSEG:
                        prep_a(nx, it, SL, ps[0:BCR, 6, 0:SL], 0)
                    state(s, it * UN + j, j)
                    if j == 0 and nx < NSEG:
                        prep_b(nx, it, SL, ps[:, 6, SL:2 * SL], 0, dl[:, nx % 2, ds(local, SL)])

            for s in range(NSEG):
                turn(s, 0)
                with dve.Fori(1, IT) as it:
                    turn(s, it)
            product(NSEG - 1, N - 1, UN - 1, 1, False)

            def last(qq, p):
                q = 2 * qq + p
                a, b_, c_, d = (4 * p + i for i in range(4))

                def s1():
                    dve.wait_ge(q_rs, q + 1)
                    dve.scalar_tensor_tensor(tt[:, p, :], u[:, ds(q * HC, HC)], chn("ln_w"), rs[:, p, :],
                                             ALU.mult, ALU.mult
                                             ).then_inc(q_t1, 1)

                def s2():
                    dve.wait_ge(q_t1, q + 1)
                    dve.scalar_tensor_tensor(tt[:, p, :], tt[:, p, :], chn("ln_b"), z[:, ds(q * HC, HC)],
                                             ALU.add, ALU.mult).then_inc(q_t, 1)

                def s3():
                    dve.wait_ge(q_rs2, q + 1)
                    dve.tensor_tensor(hn[E:128, p, :], ps[E:128, c_, :], rs[E:128, p, :], ALU.mult).then_inc(q_hn, 1)

                def s4():
                    dve.wait_ge(q_wo, q + 1)
                    opt_ge(dve, out_stored[p], 16 * qq, not isinstance(qq, int))
                    dve.scalar_tensor_tensor(ot[0:E, p, :], ps[0:E, b_, :], chn("bo", E), h1[0:E, p, :],
                                             ALU.add, ALU.add).then_inc(q_out, 1)

                return (s1, s2, s3, s4)

            both = [last(0, p) for p in range(2)]
            for st in zip(*both):
                for f in st:
                    f()
            with dve.Fori(1, Q // 2) as qq:
                both = [last(qq, p) for p in range(2)]
                for st in zip(*both):
                    for f in st:
                        f()

        @block.tensor
        def _(pe):
            pe.wait_ge(s_cb, 16)
            pe.wait_ge(onehot, 1)
            for i in range(CB):
                m = pe.matmul(ps[0:CB, 0, 0:B * NSK], cbn("ind")[:, i * CB:(i + 1) * CB],
                              oh[:, i].rearrange("p b s -> p (b s)"), start=(i == 0), stop=(i == CB - 1))
            m.then_inc(tot_ready, 1)
            pe.wait_ge(s_w, 16 * 8)
            pe.wait_ge(proj_c, 3)
            pe.matmul(ps[0:E, 7, 0:FR], pt[:, E:2 * E], tm[:], start=True, stop=True)
            for k in range(K):
                last_mm = pe.matmul(ps[:, 6, 256 + k * DI:256 + (k + 1) * DI], xd[:, k, :], dw[:, k, :],
                                    start=True, stop=True)
            last_mm.then_inc(set1, 1)
            pe.wait_ge(set1_sb, 1)
            pe.matmul(ps[:, 5, 0:FR], win[:, 0:DI], w2[:], start=True, stop=True).then_inc(set2, 1)
            pe.matmul(ps[0:FR, 7, 0:128], tm[:], pt[:], start=True, stop=True)
            pe.matmul(ps[0:FR, 7, 128 + DI:128 + 2 * DI], w2[:], win[:, DI:2 * DI], start=True, stop=True)
            pe.wait_ge(set2_sb, 1)
            pe.matmul(ps[0:FR, 7, 128:128 + DI], gx[:], cvt[:], start=True, stop=True).then_inc(set3, 1)
            pe.wait_ge(pair_ready, 1)
            pe.matmul(ps[:, 4, 0:NF * NF], con("one64", E), wpair[:].rearrange("p f g -> p (f g)"),
                      start=True, stop=True).then_inc(gram_ready, 1)
            pe.wait_ge(onehot_r, 1)
            for i in range(CB):
                m = pe.matmul(ps[0:CB, 0, 256:256 + B * NSK], con("indf")[:, i * CB:(i + 1) * CB],
                              ohq[:, i].rearrange("p b s -> p (b s)"), start=(i == 0), stop=(i == CB - 1))
            m.then_inc(tot_ready, 1)
            pe.wait_ge(tot_sb, 2)
            pe.wait_ge(set1_sb, 2)
            pe.wait_ge(set2_sb, 1)
            pe.wait_ge(gram_sb, 1)
            pe.wait_ge(s_cm, 16)
            pe.wait_ge(cmf_ready, 1)
            for w, (t_in, m_in, data, totals) in enumerate(((cbn("tri"), cm, oh, tot), (con("tri"), cmf, ohq, totr))):
                for i in range(CB):
                    dst = ps[:, 1 + i // 3, (i % 3) * B * NSK:(i % 3 + 1) * B * NSK]
                    if w == 1 and i % 3 == 0:
                        pe.wait_ge(cum_used, i // 3 + 1)
                    pe.matmul(dst, t_in, data[:, i].rearrange("p b s -> p (b s)"), start=True, stop=False)
                    m = pe.matmul(dst, m_in[:, i * 128:(i + 1) * 128], totals[:], start=False, stop=True)
                    if i % 3 == 2 or i == CB - 1:
                        m.then_inc(cum_ready, 1)
            def parts_t(v):
                for i in range(NC):
                    m = pe.transpose(ps[0:FR, i // 8, :].bitcast(BF16)[:, i % 8 * 128:(i % 8 + 1) * 128],
                                     parts[:, v, i].rearrange("p i j f -> p (i j f)"), cbn("ident"))
                    if i % 8 == 7:
                        m.then_inc(fts_ready, 1)

            pe.wait_ge(part_step, 9)
            pe.wait_ge(cum_used, 12)
            parts_t(1)

            def xz(w):
                wt = g36[:, 128 + w * DI:128 + (w + 1) * DI]
                if w == 0:
                    for i in range(4):
                        pe.wait_ge(fts_act, i // 2 + 1)
                        pe.matmul(ps[:, 4 + i, :], wt, f36[:, 1, i * HC:(i + 1) * HC], start=True, stop=True
                                  ).then_inc(xz_ready, 1)
                    pe.wait_ge(fts_dve, 2)
                with pe.Fori(1 - w, B) as b:
                    for i in range(4):
                        pe.wait_ge(xz_done, w * Q + b * 4 + i - 3)
                        pe.matmul(ps[:, 4 + i, :], wt, f36[:, 1, ds(b * L + i * HC, HC)], start=True, stop=True
                                  ).then_inc(xz_ready, 1)

            pe.wait_ge(g_step, 4)
            xz(0)
            pe.wait_ge(fts_act, 2)
            pe.wait_ge(fts_dve, 2)
            parts_t(0)

            def prep(s, u_ap, bc, dt):
                k = segment(s)[1]
                pe.matmul(bc, xb[:, k, :], u_ap, start=True, stop=True)
                pe.matmul(dt, wdt[:, k, :], u_ap, start=True, stop=True).then_inc(x_ready, 1)

            pe.wait_ge(fts_dve, 6)
            pe.wait_ge(xz_done, 2)
            for i in range(2):
                prep(0, u[:, i * HC:(i + 1) * HC], ps[0:BCR, 2 * i, :], ps[:, 1 + 2 * i, :])
            xz(1)

            def spread(s, n, h, bank, which, ready):
                s, n = (s + 1, n - N) if is_first(n) and n >= N else (s, n)
                k = segment(s)[1]
                t = phys(k, h) * HC
                pe.matmul(ps[:, bank, :], selb[0:BCR, ds(which * N + n, 1), :].rearrange("p o d -> p (o d)"),
                          pr[:, s % 2, t:t + HC], start=True, stop=True).then_inc(ready, 1)

            def spread_c(s, n, h):
                g = 2 * (s * N + n) + h
                opt_ge(pe, p_done, g - 1, not (s == 0 and is_first(n) and n == 0))
                spread(s, n, h, 4 + h, 1, c_ready)

            def add_up(s, n, j, w, start, stop=False):
                st = s * N + n
                if w == 0:
                    pe.wait_ge(p_done, 2 * st + 2)
                m = pe.matmul(ps[:, w, :], con("cen128"), pv[:, j, w * HC:(w + 1) * HC], start=start, stop=stop)
                if w == 1:
                    m.then_inc(sum_done, 1)

            def begin_y(s):
                b, k, c = segment(s)
                opt_ge(pe, y_taken, (0, 1, 0, 2)[s % 4] + 3 * (s // 4), s > 0)
                for w in range(2):
                    t = b * L + c * CH + w * HC
                    if k == 0:
                        pe.matmul(ps[:, w, :], dcen[:], u[:, t:t + HC], start=True, stop=False)
                    else:
                        pe.matmul(ps[:, w, :], con("ident"), ysv[:, w * HC:(w + 1) * HC], start=True, stop=False)

            def turn(s, it):
                nx = s + 1
                for j in range(UN):
                    n = it * UN + j
                    if j == 0 and nx < NSEG:
                        nb, nk, nc_ = segment(nx)
                        local = snapped(pe, it * SL if nk == 0 else it * -SL + (IT - 1) * SL)
                        pe.wait_ge(x_delta, prepared(nx, it))
                        prep(nx, u[:, ds(nb * L + nc_ * CH + local, SL)], ps[0:BCR, 6, 0:SL], ps[:, 6, SL:2 * SL])
                    ahead = not (s == NSEG - 1 and is_first(it) and it == IT - 1 and j >= 2)
                    for h in range(2):
                        g = 2 * (s * N + n) + h
                        if ahead:
                            if is_first(n) and n + 2 == N and h == 0:
                                pe.wait_ge(x_parts, prepared(s + 2, 0))
                            pe.wait_ge(b_copied, g + 4)
                            spread(s, n + 2, h, 7, 0, b_ready)
                        if not is_first(it) or it > 0:
                            add_up(s, n - 3, (j + 1) % UN, h, False)
                        elif j == 3:
                            if h == 0 and s % 4 != 2:
                                begin_y(s)
                            add_up(s, 0, 0, h, False)
                        elif s > 0:
                            add_up(s - 1, N - 3 + j, 1 + j, h, False, j == 2 and (s - 1) % 4 != 1)
                        if h == 1:
                            spread_c(s, n, 0)
                        elif not is_first(n) or n > 0:
                            spread_c(s, n - 1, 1)
                        elif s > 0:
                            spread_c(s - 1, N - 1, 1)

            pe.wait_ge(sel_ready, 1)
            pe.wait_ge(x_parts, 2)
            pe.wait_ge(x_delta, 2)
            pe.wait_ge(xz_done, 2 * Q)
            pe.wait_ge(dcen_ready, 1)
            for g in range(4):
                opt_ge(pe, b_copied, g, g > 0)
                spread(0, g // 2, g % 2, 7, 0, b_ready)
            for s in range(NSEG):
                turn(s, 0)
                with pe.Fori(1, IT - 1) as it:
                    turn(s, it)
                turn(s, IT - 1)
            spread_c(NSEG - 1, N - 1, 1)
            for j in (1, 2, 3):
                for w in range(2):
                    add_up(NSEG - 1, N - UN + j, j, w, False, j == 3)

            def last(qq, p):
                q = 2 * qq + p
                a, b_, c_, d = (4 * p + i for i in range(4))

                def s2():
                    pe.wait_ge(q_sq, q + 1)
                    if not isinstance(qq, int) or q >= 2:
                        pe.wait_ge(q_out, q - 1)
                    pe.matmul(ps[:, b_, :], con("one128"), sq[:, p, :], start=True, stop=True).then_inc(q_var, 1)

                def s3():
                    pe.wait_ge(q_t, q + 1)
                    pe.matmul(ps[:, c_, :], wou[:], tt[:, p, :], start=True, stop=False)
                    pe.matmul(ps[:, c_, :], g36[:, 0:128], f36[:, 0, ds(q * HC, HC)], start=False, stop=True
                              ).then_inc(q_o, 1)

                def s5():
                    pe.wait_ge(q_sq2, q + 1)
                    pe.matmul(ps[:, b_, :], con("one64")[E:128, :], sq[E:128, p, :], start=True, stop=True
                              ).then_inc(q_var2, 1)

                def s6():
                    pe.wait_ge(q_hn, q + 1)
                    pe.matmul(ps[:, a, :], wi_[E:128, :], hn[E:128, p, :], start=True, stop=True).then_inc(q_w, 1)

                def layer(l, src, bank, ready, done):
                    def f():
                        pe.wait_ge(ready, q + 1)
                        if l == 0:
                            pe.wait_ge(we_loaded[p], 16 * GQ * (qq + 1))
                        pe.matmul(ps[:, bank, :].rearrange("p (g t) -> p g t", t=TG), brp[:, l * HID:(l + 1) * HID],
                                  ohr[:, ds(q * GQ, GQ)].unsqueeze(2).to_broadcast([BR, GQ, TG]),
                                  start=True, stop=False)
                        for g in range(GQ):
                            m = pe.matmul(ps[:, bank, g * TG:(g + 1) * TG], we[:, p * GQ + g, l, :],
                                          src[:, p, g * TG:(g + 1) * TG], start=False, stop=(g == GQ - 1))
                        m.then_inc(done, 1)
                    return f

                def s9():
                    pe.wait_ge(q_f2, q + 1)
                    pe.matmul(ps[:, b_, :], wo_[:], fa[:, p, :], start=True, stop=True).then_inc(q_wo, 1)

                return (s2, s3, s5, s6, layer(0, fa, c_, q_f0, q_l0), layer(1, fb, d, q_f1, q_l1), s9)

            pe.wait_ge(bias_step, 5)
            pe.wait_ge(wou_step, 3)
            both = [last(0, p) for p in range(2)]
            for st in zip(*both):
                for f in st:
                    f()
            with pe.Fori(1, Q // 2) as qq:
                both = [last(qq, p) for p in range(2)]
                for st in zip(*both):
                    for f in st:
                        f()


def constants():
    import numpy as np
    cf = np.zeros((128, CFW), np.float32)

    def put(name, a):
        cf[:a.shape[0], CF[name][0]:CF[name][0] + a.shape[1]] = a

    i = np.arange(128)
    eye = np.eye(128, dtype=np.float32)
    put("ident", eye)
    put("tri", (i[:, None] <= i[None, :]).astype(np.float32))
    put("cen128", eye - np.float32(1 / DI))
    put("one128", np.full((128, 128), 1 / DI, np.float32))
    put("one64", np.full((128, 128), 1 / E, np.float32))
    put("iota", np.tile(np.arange(NSK, dtype=np.float32), (128, 1)))

    def part_masks(part):
        return np.stack([-1.0 * (part >= 1), -1.0 * (part >= 2)], 1).astype(np.float32)

    put("m36", part_masks(np.arange(FR) // NF % 3))
    r = np.arange(BCR)
    put("mbc", part_masks((r % 64) // N))
    r = np.arange(BR)
    put("mbr", part_masks(r // 32))
    e = r % 32
    put("eid", np.stack([np.where(e < NX, e, -1e9), 1.0 * (e == NX)], 1).astype(np.float32))
    put("indf", np.tile(np.eye(CB, dtype=np.float32).reshape(1, -1), (128, 1)))
    sel = np.zeros((128, 2 * N), np.float32)
    for w in range(2):
        for n in range(N):
            for part in range(3):
                sel[64 * w + part * N + n, w * N + n] = 1.0
    put("sel", sel)
    cm = (np.arange(CB)[:, None, None] < np.arange(CB)[None, :, None]) * np.ones((1, 1, 128))
    cb = np.concatenate([cf[:, slice(*CF[n])] for n in ("tri", "indf", "ident")], 1)
    one = 0x3F80
    return cf, (cb * one).astype(np.uint16), (cm.reshape(CB, CB * 128) * one).astype(np.uint16)


def kernel(**inputs):
    import numpy as np
    import concourse.bacc as _bacc
    from concourse.bass_utils import run_bass_kernel_spmd as _run

    x = {n: np.asarray(v) for n, v in inputs.items()}
    a = {n[8:]: v for n, v in x.items() if n.startswith("L0_attn_")}
    f = {n[7:]: v for n, v in x.items() if n.startswith("L0_ffn_")}
    t = {n[7:]: v for n, v in x.items() if n.startswith("L0_tok_")}
    f32 = np.float32

    def toks(v):
        return v.reshape(B, CB, 128).transpose(2, 0, 1).reshape(128, NC)

    def col(v):
        return np.concatenate([v, np.zeros(128 - v.shape[0], f32)])

    cf, cb, cm = constants()
    m = np.zeros((E + 1, NF), f32)
    n0, n1 = t["skill_w"].shape[0], t["skill_w"].shape[0] + t["att_w"].shape[0]
    m[0:n0, 0], m[n0:n1, 1], m[n1:E, 2] = t["skill_w"], t["att_w"], t["mast_w"]
    m[0:n0, 3], m[n0:n1, 3], m[n1:E, 3] = t["skill_b"], t["att_b"], t["mast_b"]
    m[E, 3] = 1.0
    xp = a["x_proj_w"]
    xbc = np.zeros((DI, K, BCR), f32)
    for part in range(3):
        xbc[:, :, part * N:(part + 1) * N] = xp[:, R:R + N].transpose(2, 0, 1)
        xbc[:, :, 64 + part * N:64 + (part + 1) * N] = xp[:, R + N:R + 2 * N].transpose(2, 0, 1)
    bb = np.concatenate([f["br"].transpose(1, 0, 2), f["bs"].transpose(1, 0, 2)], 0).reshape(NX + 1, NL * HID)
    route = f["route_id"].reshape(1, NR)
    arrays = {
        "tok": np.stack([toks(x["x"]), toks(x["mask_BS_i0_1"])], 1),
        "consts": cf, "constb": cb, "cmask": cm,
        "chan": np.stack([a["conv_b"], a["dt_b"][0], a["dt_b"][1], a["Ds"][:DI], a["Ds"][DI:], a["ln_w"], a["ln_b"],
                          f["bi"], col(f["bo"])], 1),
        "tokm": np.tile(m, (1, FR // NF)),
        "projt": np.pad(np.concatenate([t["proj_w"].T, t["proj_b"][None]], 0), ((0, 0), (0, 128 - E))),
        "wint": a["W_in"].T, "convt": a["conv_w"].T, "xbc": xbc,
        "xdt": xp[:, :R].transpose(1, 0, 2), "dtw": a["dt_w"].transpose(2, 0, 1),
        "alog": a["A_logs"].reshape(K, DI, N).transpose(1, 0, 2).reshape(DI, K * N),
        "wout": np.pad(a["W_out"].T, ((0, 0), (0, 128 - E))), "wit": np.pad(f["Wi"].T, ((128 - E, 0), (0, 0))), "ws": f["Ws"][:, 0].transpose(2, 0, 1), "wo": np.pad(f["Wo"].T, ((0, 0), (0, 128 - E))),
        "wr": f["Wr"].transpose(1, 3, 0, 2), "brb": np.tile(np.pad(bb, ((0, 31 - NX), (0, 0))), (3, 1)), "route": route, "routeb": np.tile(route, (BR, 1)),
    }
    arrays = {n: np.ascontiguousarray(v) for n, v in arrays.items()}
    nc = _bacc.Bacc("TRN2", target_bir_lowering=False, num_devices=1)
    args = [nc.dram_tensor(n, v.shape, mybir.dt.from_np(v.dtype), kind="ExternalInput").ap()
            for n, v in arrays.items()]
    args.append(nc.dram_tensor("wsum", (NX + 1, HID, NL, HID), F32, kind="Internal").ap())
    args.append(nc.dram_tensor("h_t", (E, T), F32, kind="ExternalOutput").ap())
    bass_lm_tower(nc, *args)
    r = _run(nc, [arrays], core_ids=[0])
    return np.ascontiguousarray(r.results[0]["h_t"].T).reshape(B, L, E)
```

```python
from contextlib import ExitStack

import concourse.bass as bass
from concourse import mybir

F32 = mybir.dt.float32
BF16 = mybir.dt.bfloat16
I32 = mybir.dt.int32
U16 = mybir.dt.uint16
ALU = mybir.AluOpType
ACT = mybir.ActivationFunctionType
AX = mybir.AxisListType
ds = bass.ds

B, L = 2, 2048
NSK = 75
E = 64
DI = 128
K = 2
N = 16
R = 16
HID = 128
NX = 16
NL = 2
NR = 64
TG = B * L // NR
T = B * L
NC = T // 128
CB = L // 128
CH = 1024
HC = 512
SL = 256
NSEG = B * K * (L // CH)
UN = 4
IT = N // UN
NF = 4
FR = 3 * 3 * NF
BR = 96
BCR = 112
EPS = 1e-5
BIG = 1e17
Q = T // HC
GQ = HC // TG

CF = {}
_at = 0
for _n, _w in (("iota", NSK), ("ident", 128), ("tri", 128), ("cen128", 128), ("one128", 128), ("one64", 128),
               ("m36", 2), ("mbc", 2), ("mbr", 2), ("eid", 2), ("indf", CB * CB), ("sel", 2 * N)):
    CF[_n] = (_at, _at + _w)
    _at += _w
CFW = _at
CBF = {"tri": (0, 128), "ind": (128, 128 + CB * CB), "ident": (128 + CB * CB, 256 + CB * CB)}
CBW = 256 + CB * CB
CHN = ["conv_b", "dt_b0", "dt_b1", "d0", "d1", "ln_w", "ln_b", "bi", "bo"]


def segment(s):
    b, r = divmod(s, 4)
    return b, (0, 0, 1, 1)[r], (0, 1, 1, 0)[r]


def bass_lm_tower(nc, tok, consts, constb, cmask, chan, tokm, projt, wint, convt, xbc, xdt, dtw, alog, wout, wit,
                  ws, wo, wr, brb, route, routeb, wsum, out):
    with ExitStack() as ctx:
        def sb(name, shape, dt=F32):
            return ctx.enter_context(nc.sbuf_tensor(name, shape, dt))

        def sem(name):
            return ctx.enter_context(nc.semaphore(name))

        ps = ctx.enter_context(nc.psum_tensor("ps", [128, 8, 512], F32))

        cf = sb("cf", [128, CFW])
        cbf = sb("cbf", [128, CBW], BF16)
        cm = sb("cm", [CB, CB * 128], BF16)
        ch = sb("ch", [128, len(CHN)])
        tm = sb("tm", [E + 1, FR])
        pt = sb("pt", [E + 1, 128])
        pmean = sb("pmean", [DI, 4])
        win = sb("win", [E, 2 * DI])
        cvt = sb("cvt", [DI, DI])
        xb = sb("xb", [DI, K, BCR])
        xd = sb("xd", [R, K, DI])
        dw = sb("dw", [R, K, DI])
        wdt = sb("wdt", [DI, K, DI])
        al = sb("al", [DI, K * N])
        na = sb("na", [DI, K * N])
        wou = sb("wou", [DI, 128])
        wi_ = sb("wi_", [128, HID])
        si = sb("si", [HID, NL, HID])
        wo_ = sb("wo_", [HID, 128])
        br = sb("br", [BR, NL * HID])
        brr = sb("brr", [BR, NL * HID])
        brh = sb("brh", [BR, NL * HID], BF16)
        brp = sb("brp", [BR, NL * HID], BF16)
        rtb = sb("rtb", [BR, NR], I32)
        ohr = sb("ohr", [BR, NR], BF16)
        rt = sb("rt", [1, NR], I32)
        rtw = sb("rtw", [1, 4, NR])
        slot = sb("slot", [1, NR], I32)
        selb = sb("selb", [128, 2 * N, 128], BF16)
        dsum = sb("dsum", [DI, 1])
        eps = sb("eps", [128, 1])
        ysv = sb("ysv", [DI, CH])

        tk = sb("tk", [128, 2, NC], I32)
        tf = sb("tf", [128, 2, NC])
        cmf = sb("cmf", [CB, CB * 128])
        tot = sb("tot", [CB, B * NSK], BF16)
        totr = sb("totr", [CB, B * NSK])
        f2 = sb("f2", [128, 2, NF * NC])
        ft = f2[:, 0, :].rearrange("p (f c) -> p f c", f=NF)
        ftn = f2[:, 1, :].rearrange("p (f c) -> p f c", f=NF)
        val = sb("val", [128, 3, NC])
        ss = sb("ss", [128, 3, NC])
        outer = sb("outer", [128, NF * NF, NC])
        outg = sb("outg", [128, NF * NF, NC])
        gram = sb("gram", [128, NF * NF])
        wpair = sb("wpair", [E, NF, NF])
        parts = sb("parts", [128, 2, NC, 3, 3, NF], BF16)
        rest = sb("rest", [128, 2, NF * NC])
        w2 = sb("w2", [E, FR])
        gx = sb("gx", [DI, FR])
        GC = 3 * 128
        gwr = sb("gwr", [FR, GC])
        gwh = sb("gwh", [FR, 2, GC], BF16)
        g36 = sb("g36", [FR, GC], BF16)
        f36 = sb("f36", [FR, 2, T], BF16)

        u = sb("u", [DI, T])
        z = sb("z", [DI, T])
        wall = z[:].rearrange("p (x l j) -> p x l j", x=NX, l=NL)
        dcen = sb("dcen", [DI, DI])
        dl = sb("dl", [DI, 2, CH])
        du = sb("du", [DI, 2, CH])
        pr = sb("pr", [BCR, 2, CH], BF16)
        xe = sb("xe", [DI, CH])
        xl = sb("xl", [DI, CH])
        xh = sb("xh", [BCR, CH], BF16)
        xr = sb("xr", [BCR, CH])
        xm = sb("xm", [BCR, CH], BF16)
        carry = sb("carry", [DI, N])
        big = sb("big", [128, 5 * UN // 2 * CH + 512])
        oh = big[:, 0:1200].bitcast(BF16).rearrange("p (c b s) -> p c b s", c=CB, b=B)
        ohq = big[:, 1200:3600].rearrange("p (c b s) -> p c b s", c=CB, b=B)
        prod = big[:, 3600:8400].rearrange("p (w c b s) -> p w c b s", w=2, c=CB, b=B)
        bv = big[:, 0:UN * CH].rearrange("p (r t) -> p r t", r=UN)
        pv = big[:, UN * CH:2 * UN * CH].rearrange("p (r t) -> p r t", r=UN)
        hv = big[:, 2 * UN * CH:2 * UN * CH + 2 * CH].rearrange("p (r t) -> p r t", r=2)
        sq, rs, tt, hn, fa, fb, fc = (big[:, 2 * HC * w:2 * HC * (w + 1)].rearrange("p (r t) -> p r t", r=2)
                                      for w in range(7))
        sq0, rs0, tt0, h0 = (x[:, w * HC:(w + 1) * HC] for x in (xe, xl) for w in range(2))
        hn0, fa0 = du[:, 0, 0:HC], dl[:, 0, :].rearrange("p (r t) -> p r t", r=2)
        wes = sb("wes", [HID, 2 * GQ * NL * HID])
        we = wes[:].rearrange("p (r l j) -> p r l j", r=2 * GQ, l=NL)

        s_tok, s_con, s_cm, s_w, s_late = (sem(n) for n in (
            "tok_loaded", "consts_loaded", "cmask_loaded", "weights_loaded", "late_loaded"))
        s_iota = sem("iota_loaded")
        s_cb, s_si, s_wall, wall_summed, wsum_stored = (sem(n) for n in (
            "constb_loaded", "shared_loaded", "experts_in", "experts_summed", "experts_stored"))
        cmf_ready, sel_ready, neg_a, exp_a = sem("cmf_ready"), sem("sel_ready"), sem("neg_a"), sem("exp_a")
        proj_c, set1, set1_sb, set2, set2_sb, set3 = (sem(n) for n in (
            "proj_centred", "setup1", "setup1_copied", "setup2", "setup2_copied", "setup3"))
        g_step, bias_step, route_step, dsum_ready, dcen_ready, si_ready = (sem(n) for n in (
            "g_step", "bias_step", "route_step", "dsum_ready", "dcen_ready", "si_ready"))
        pair_ready, gram_ready, gram_sb, wou_step = (sem(n) for n in (
            "pair_ready", "gram_ready", "gram_copied", "wou_step"))
        tok_f, onehot, onehot_r, tot_ready, tot_sb, cum_ready, cum_used = (sem(n) for n in (
            "tok_float", "onehot", "onehot_r", "totals", "totals_copied", "cum_ready", "cum_used"))
        feat, ss_ready, rstd_ready = (sem(n) for n in ("features", "ss_ready", "rstd_ready"))
        eps_set = sem("eps_set")
        part_step, fts_ready, fts_copied = (sem(n) for n in ("part_step", "parts_t", "parts_t_copied"))
        xz_ready, xz_done = sem("xz_ready"), sem("xz_done")
        x_ready, x_exp, x_hi, x_min, x_rest, x_ln, x_mid, x_parts, x_delta, x_du = (sem(n) for n in (
            "x_ready", "x_exp", "x_hi", "x_min", "x_rest", "x_ln", "x_mid", "x_parts", "x_delta", "x_du"))
        b_ready, b_copied, c_ready, a_ready, mul_done, scan_done = (sem(n) for n in (
            "b_ready", "b_copied", "c_ready", "a_ready", "mul_done", "scan_done"))
        h0_saved = sem("h0_saved")
        p_done, sum_done, y_taken = (sem(n) for n in (
            "p_done", "sum_done", "y_taken"))
        q_sq, q_var, q_ln, q_rs, q_t1, q_t, q_o = (sem(n) for n in (
            "y_squared", "y_var", "y_ln", "y_rstd", "y_scaled", "y_gated", "o_ready"))
        q_sq2, q_var2, q_ln2, q_rs2, q_hn, q_w, q_f0, q_l0, q_f1, q_l1, q_f2, q_wo, q_out = (
            sem(n) for n in ("h1_squared", "h1_var", "h1_ln", "h1_rstd", "h1_normed", "wi_ready", "f0_ready",
                             "l0_ready", "f1_ready", "l1_ready", "f2_ready", "wo_ready", "out_ready"))
        we_loaded = [[sem(f"experts_loaded{p}{half}") for half in range(2)] for p in range(2)]
        out_stored = sem("out_stored")

        W2, WDT = slice(0, FR), slice(FR, FR + K * DI)
        GX, GRAM = slice(WDT.stop, WDT.stop + FR), slice(WDT.stop + FR, WDT.stop + FR + NF * NF)

        def con(name, rows=128):
            a, b_ = CF[name]
            return cf[0:rows, a:b_]

        def chn(name, rows=128):
            i = CHN.index(name)
            return ch[0:rows, i:i + 1]

        def cb_view(ap):
            return ap.rearrange("p (b c) -> p c b", b=B)

        def prepared(s, it):
            return it if s == 0 else 2 + (s - 1) * IT + it

        def slice_at(s, it):
            b, k, c = segment(s)
            return b * L + c * CH + (it * SL if k == 0 else it * -SL + (IT - 1) * SL)

        def phys(k, h):
            return h if k == 0 else 1 - h

        def cbn(name, rows=128):
            a, b_ = CBF[name]
            return cbf[0:rows, a:b_]

        def known(v):
            return isinstance(v, int)

        def opt_ge(eng, s, v, ok):
            if ok:
                eng.wait_ge(s, v)

        def snapped(eng, v):
            return v if isinstance(v, int) else eng.snap(v)

        def experts(eng, q, p, half):
            for i in range(GQ // 2):
                g = half * (GQ // 2) + i
                e = eng.value_load(slot[0:1, ds(q * GQ + g, 1)], min_val=0, max_val=NX)
                eng.dma_start(we[:, p * GQ + g, :, :], wsum[ds(e, 1)].rearrange("o i l j -> i (o l) j")
                              ).then_inc(we_loaded[p][half], 16)

        def prep_parts(eng, s, it, width, o, local):
            eng.wait_ge(x_mid, prepared(s, it) + 1)
            eng.tensor_tensor(pr[:, s % 2, ds(local, width)], xm[:, o:o + width], xr[:, o:o + width], ALU.add
                              ).then_inc(x_parts, 1)

        def prep_du(eng, s, it, width, local, t0):
            eng.wait_ge(x_delta, prepared(s, it) + 1)
            eng.tensor_tensor(du[:, s % 2, ds(local, width)], dl[:, s % 2, ds(local, width)], u[:, ds(t0, width)],
                              ALU.mult).then_inc(x_du, 1)

        bank_in, bank_var, bank_h1, bank_ffn = (0, 4), (2, 5), (1, 6), (3, 7)

        block = ctx.enter_context(nc.Block())

        @block.sync
        def _(sp):
            sp.dma_start(tk[:], tok).then_inc(s_tok, 16)
            sp.dma_start(cf[:, 0:NSK], consts[:, 0:NSK]).then_inc(s_iota, 16)
            sp.dma_start(cbf[:], constb.bitcast(BF16)).then_inc(s_cb, 16)
            sp.dma_start(cm[:], cmask.bitcast(BF16)).then_inc(s_cm, 16)
            sp.dma_start(cf[:, NSK:CFW], consts[:, NSK:CFW]).then_inc(s_con, 16)
            sp.dma_start(si[:], ws).then_inc(s_si, 16)
            for dst, src in ((al, alog), (wou, wout), (wi_, wit), (wo_, wo), (br, brb), (rtb, routeb), (rt, route)):
                sp.dma_start(dst[:], src).then_inc(s_late, 16)
            sp.dma_start(wall, wr.rearrange("x i l j -> i x l j")).then_inc(s_wall, 16)
            sp.wait_ge(si_ready, 1)
            sp.wait_ge(wall_summed, 1)
            sp.dma_start(wsum[0:NX].rearrange("x i l j -> i x l j"), wall).then_inc(wsum_stored, 16)
            sp.dma_start(wsum[NX], si[:]).then_inc(wsum_stored, 16)

            sp.wait_ge(route_step, 5)
            sp.wait_ge(wsum_stored, 32)
            for q in range(2):
                experts(sp, q, q, 0)
            with sp.Fori(0, Q // 2 - 1) as qq:
                for p in range(2):
                    sp.wait_ge(q_l1, 2 * qq + p + 1)
                    experts(sp, 2 * qq + p + 2, p, 0)
                for p in range(2):
                    sp.wait_ge(q_out, 2 * qq + p + 1)
                    sp.dma_start(out[:, ds((2 * qq + p) * HC, HC)], z[0:E, ds((2 * qq + p) * HC, HC)]
                                 ).then_inc(out_stored, 16)
            for q in (Q - 2, Q - 1):
                sp.wait_ge(q_out, q + 1)
                sp.dma_start(out[:, q * HC:(q + 1) * HC], z[0:E, q * HC:(q + 1) * HC]).then_inc(out_stored, 16)
            sp.wait_ge(out_stored, 16 * Q)

        @block.gpsimd
        def _(pool):
            pool.wait_ge(s_cm, 16)
            pool.tensor_copy(cmf[:], cm[:]).then_inc(cmf_ready, 1)
            pool.wait_ge(s_con, 16)
            pool.wait_ge(si_ready, 1)
            pool.wait_ge(s_wall, 16)
            pool.tensor_tensor(wall, wall, si[:].unsqueeze(1).to_broadcast([HID, NX, NL, HID]), ALU.add
                               ).then_inc(wall_summed, 1)
            pool.tensor_copy(selb[:], con("sel").unsqueeze(2).to_broadcast([128, 2 * N, 128])).then_inc(sel_ready, 1)
            pool.wait_ge(route_step, 5)
            pool.wait_ge(wsum_stored, 32)
            for q in range(2):
                experts(pool, q, q, 1)

            def product(s, it, j):
                st = s * N + it * UN + j
                pool.wait_ge(b_copied, 2 * st + 2)
                pool.tensor_tensor(bv[:, j, :], bv[:, j, :], du[:, s % 2, :], ALU.mult).then_inc(mul_done, 1)

            def turn(s, it):
                nx = s + 1
                if nx < NSEG:
                    nb, nk, nc_ = segment(nx)
                    local = snapped(pool, it * SL if nk == 0 else it * -SL + (IT - 1) * SL)
                for j in range(UN):
                    product(s, it, j)
                    if j == 1 and nx < NSEG:
                        prep_parts(pool, nx, it, SL, 0, local)
                    if j == 2 and nx < NSEG:
                        prep_du(pool, nx, it, SL, local, nb * L + nc_ * CH + local)

            for s in range(NSEG):
                pool.wait_ge(x_du, prepared(s + 1, 0))
                turn(s, 0)
                with pool.Fori(1, IT) as it:
                    turn(s, it)
            with pool.Fori(0, Q // 2 - 1) as qq:
                for p in range(2):
                    pool.wait_ge(q_l1, 2 * qq + p + 1)
                    experts(pool, 2 * qq + p + 2, p, 1)

        @block.scalar
        def _(act):
            for dst, src in ((tm, tokm), (pt, projt), (win, wint), (cvt, convt), (xb, xbc), (xd, xdt), (dw, dtw),
                             (ch, chan)):
                act.dma_start(dst[:], src).then_inc(s_w, 16)
            act.wait_ge(tot_ready, 1)
            act.activation(tot[:], ps[0:CB, 0, 0:B * NSK], ACT.Copy).then_inc(tot_sb, 1)
            act.preload_act_table_set("natural_log_exp_and_others")
            act.wait_ge(tot_ready, 2)
            act.activation(totr[:], ps[0:CB, 0, 256:256 + B * NSK], ACT.Copy).then_inc(tot_sb, 1)
            act.wait_ge(set1, 1)
            act.activation(w2[:], ps[0:E, 7, W2], ACT.Copy).then_inc(set1_sb, 1)
            act.activation(wdt[:], ps[:, 7, WDT].rearrange("p (k d) -> p k d", k=K), ACT.Copy).then_inc(set1_sb, 1)
            act.wait_ge(set2, 1)
            act.activation(gx[:], ps[:, 7, GX], ACT.Copy).then_inc(set2_sb, 1)
            act.activation(gram[:], ps[:, 7, GRAM], ACT.Copy).then_inc(gram_sb, 1)
            act.wait_ge(s_late, 16 * 7)
            act.activation(na[:], al[:], ACT.Exp).then_inc(exp_a, 1)
            act.wait_ge(exp_a, 1)
            act.activation(na[:], na[:], ACT.Copy, scale=-1.0).then_inc(neg_a, 1)
            act.wait_ge(ss_ready, 4)
            act.activation(ss[:, 2, :], ss[:, 1, :], ACT.Ln).then_inc(rstd_ready, 1)
            act.wait_ge(rstd_ready, 1)
            act.activation(ss[:, 0, :], ss[:, 2, :], ACT.Exp, scale=-0.5).then_inc(rstd_ready, 1)
            act.preload_act_table_set("silu_and_others")
            for w, (dst, bias) in enumerate(((u, chn("conv_b")), (z, 0.0))):
                if w == 1:
                    act.wait_ge(wsum_stored, 32)
                for i in range(Q):
                    act.wait_ge(xz_ready, w * Q + i + 1)
                    act.activation(dst[:, i * HC:(i + 1) * HC], ps[:, 4 + i % 4, :], ACT.Silu, bias=bias
                                   ).then_inc(xz_done, 1)
            act.preload_act_table_set("natural_log_exp_and_others")

            def prep_exp(s, it, t0, width, bank, bc, o):
                _, k, _ = segment(s)
                act.wait_ge(x_ready, prepared(s, it) + 1)
                act.activation(xe[:, o:o + width], bank[:, :], ACT.Exp, bias=chn(f"dt_b{k}")).then_inc(x_exp, 1)
                act.activation(xh[:, o:o + width], bc, ACT.Identity, scale=con("mbc", BCR)[:, 0:1]).then_inc(x_hi, 1)

            def prep_ln(s, it, width, o):
                act.wait_ge(x_min, prepared(s, it) + 1)
                act.activation(xl[:, o:o + width], xe[:, o:o + width], ACT.Ln, bias=1.0).then_inc(x_ln, 1)
                act.wait_ge(x_rest, prepared(s, it) + 1)
                act.activation(xm[:, o:o + width], xr[:, o:o + width], ACT.Identity, scale=con("mbc", BCR)[:, 1:2]
                               ).then_inc(x_mid, 1)

            for i in range(2):
                prep_exp(0, i, i * HC, HC, ps[:, 1 + 2 * i, :], ps[0:BCR, 2 * i, :], i * HC)
            for i in range(2):
                prep_ln(0, i, HC, i * HC)

            def copy_b(s, n, j, h, bank=7):
                s, n = (s + 1, n - N) if known(n) and n >= N else (s, n)
                g = 2 * (s * N + n) + h
                t = phys(segment(s)[1], h) * HC
                act.wait_ge(b_ready, g + 1)
                act.activation(bv[:, j, t:t + HC], ps[:, bank, :], ACT.Copy).then_inc(b_copied, 1)

            def save_carry(s, n, j):
                if s % 2 == 0:
                    e = CH - 1 if segment(s)[1] == 0 else 0
                    act.activation(carry[:, ds(n, 1)], hv[:, j % 2, e:e + 1], ACT.Copy)

            def state(s, n, j, ahead, after):
                _, k, _ = segment(s)
                for h in range(2):
                    g = 2 * (s * N + n) + h
                    t = phys(k, h) * HC
                    opt_ge(act, scan_done, g - 1, not (s == 0 and known(n) and n == 0))
                    if ahead:
                        copy_b(s, n + 2, (j + 2) % UN, h)
                    if h == 0:
                        if not known(n) or n >= 2:
                            save_carry(s, n - 2, j)
                        elif s > 0:
                            save_carry(s - 1, N - 2 + n, j)
                    act.activation(ps[:, 2 + h, :], dl[:, s % 2, t:t + HC], ACT.Exp,
                                   scale=na[:, ds(k * N + n, 1)]).then_inc(a_ready, 1)
                    after(h)

            def take_y(s, w):
                b, k, c = segment(s)
                t = b * L + c * CH + w * HC
                act.wait_ge(sum_done, 2 * N * (s + 1) - 1 + w)
                act.activation(ysv[:, w * HC:(w + 1) * HC] if s % 4 == 0 else u[:, t:t + HC], ps[:, w, :], ACT.Copy
                               ).then_inc(y_taken, 1)

            def turn(s, it):
                def after(j, h):
                    if j == 0 and s + 1 < NSEG:
                        if h == 0:
                            prep_exp(s + 1, it, None, SL, ps[:, 6, SL:2 * SL], ps[0:BCR, 6, 0:SL], 0)
                        else:
                            prep_ln(s + 1, it, SL, 0)
                    if known(it) and it == 0 and j == 2 and s > 0 and (s - 1) % 4 != 1:
                        take_y(s - 1, h)
                    if s == NSEG - 1:
                        early(it * UN + j, h)

                for j in range(UN):
                    state(s, it * UN + j, j, not (s == NSEG - 1 and known(it) and it == IT - 1 and j >= 2),
                          lambda h: after(j, h))

            def squares(qq):
                for p in range(2):
                    q = 2 * qq + p
                    act.activation(sq[:, p, :], u[:, q * HC:(q + 1) * HC], ACT.Square).then_inc(q_sq, 1)

            def first_relu(q):
                act.wait_ge(q_w, q + 1)
                act.activation(fa0[:, q, :], ps[:, (6, 4)[q], :], ACT.Relu, bias=chn("bi")).then_inc(q_f0, 1)

            def early(n, h):
                for q in range(2):
                    step = (n - 8 * q, h)
                    if step == (0, 1):
                        if q == 0:
                            act.wait_ge(y_taken, 6)
                        else:
                            act.wait_ge(q_var2, q)
                        act.activation(sq0, u[:, q * HC:(q + 1) * HC], ACT.Square).then_inc(q_sq, 1)
                    elif step == (2, 0):
                        opt_ge(act, q_hn, q, q > 0)
                        act.wait_ge(q_var, q + 1)
                        act.activation(rs0, ps[:, 6, :], ACT.Ln, bias=eps[:, 0:1]).then_inc(q_ln, 1)
                    elif step == (2, 1):
                        act.wait_ge(q_ln, q + 1)
                        act.activation(rs0, rs0, ACT.Exp, scale=-0.5).then_inc(q_rs, 1)
                    elif step == (6, 0):
                        act.wait_ge(q_o, q + 1)
                        act.activation(z[0:E, q * HC:(q + 1) * HC], ps[0:E, 6, :], ACT.Copy)
                        act.activation(h0[E:128, :], ps[E:128, 6, :], ACT.Copy).then_inc(h0_saved, 1)
                    elif step == (6, 1):
                        act.wait_ge(h0_saved, q + 1)
                        act.activation(sq0[E:128, :], h0[E:128, :], ACT.Square).then_inc(q_sq2, 1)
                    elif step == (8, 0):
                        act.wait_ge(q_var2, q + 1)
                        act.activation(rs0[E:128, :], ps[E:128, 6, :], ACT.Ln, bias=eps[E:128, 0:1]).then_inc(q_ln2, 1)
                        act.wait_ge(q_ln2, q + 1)
                        act.activation(rs0[E:128, :], rs0[E:128, :], ACT.Exp, scale=-0.5).then_inc(q_rs2, 1)
                if (n, h) == (11, 0):
                    first_relu(0)

            act.wait_ge(neg_a, 1)
            act.wait_ge(eps_set, 1)
            for g in range(4):
                copy_b(0, g // 2, g // 2, g % 2, 7 - g)
            act.wait_ge(x_delta, 2)
            for s in range(NSEG):
                act.wait_ge(x_delta, prepared(s + 1, 0))
                turn(s, 0)
                if s < NSEG - 1:
                    with act.Fori(1, IT - 1) as it:
                        turn(s, it)
                else:
                    for it in range(1, IT - 1):
                        turn(s, it)
                turn(s, IT - 1)
            early(N, 0)
            act.wait_ge(scan_done, 2 * N * (NSEG - 1) + 2 * (N - UN) + 2)
            squares(1)
            for w in range(2):
                take_y(NSEG - 1, w)

            def rstd(qq):
                for p in range(2):
                    act.wait_ge(q_var, 2 * qq + p + 1)
                    act.activation(rs[:, p, :], ps[:, bank_var[p], :], ACT.Ln, bias=eps[:, 0:1]).then_inc(q_ln, 1)
                for p in range(2):
                    act.wait_ge(q_ln, 2 * qq + p + 1)
                    act.activation(rs[:, p, :], rs[:, p, :], ACT.Exp, scale=-0.5).then_inc(q_rs, 1)

            def save_h1(qq):
                for p in range(2):
                    act.wait_ge(q_o, 2 * qq + p + 1)
                    act.activation(sq[E:128, p, :], ps[E:128, bank_h1[p], :], ACT.Square).then_inc(q_sq2, 1)
                for p in range(2):
                    act.activation(z[0:E, ds((2 * qq + p) * HC, HC)], ps[0:E, bank_h1[p], :], ACT.Copy)

            def rstd2(qq):
                for p in range(2):
                    act.wait_ge(q_var2, 2 * qq + p + 1)
                    act.activation(rs[E:128, p, :], ps[E:128, bank_var[p], :], ACT.Ln, bias=eps[E:128, 0:1]
                                   ).then_inc(q_ln2, 1)
                for p in range(2):
                    act.wait_ge(q_ln2, 2 * qq + p + 1)
                    act.activation(rs[E:128, p, :], rs[E:128, p, :], ACT.Exp, scale=-0.5).then_inc(q_rs2, 1)

            def relu_in(qq):
                for p in range(2):
                    act.wait_ge(q_w, 2 * qq + p + 1)
                    act.activation(fa[:, p, :], ps[:, bank_in[p], :], ACT.Relu, bias=chn("bi")).then_inc(q_f0, 1)

            def relu0(q, p):
                act.wait_ge(q_l0, q + 1)
                act.activation(fb[:, p, :], ps[:, bank_ffn[p], :], ACT.Relu).then_inc(q_f1, 1)

            def relu1(q, p):
                act.wait_ge(q_l1, q + 1)
                act.activation(fc[:, p, :], ps[:, bank_ffn[p], :], ACT.Relu).then_inc(q_f2, 1)

            first_relu(1)
            act.wait_ge(y_taken, 12)
            for qq in range(Q // 2 - 1):
                rstd(qq + 1)
                relu0(2 * qq, 0)
                relu0(2 * qq + 1, 1)
                relu1(2 * qq, 0)
                save_h1(qq + 1)
                relu1(2 * qq + 1, 1)
                rstd2(qq + 1)
                if qq + 2 < Q // 2:
                    squares(qq + 2)
                relu_in(qq + 1)
            for p in range(2):
                relu0(Q - 2 + p, p)
            for p in range(2):
                relu1(Q - 2 + p, p)

        @block.vector
        def _(dve):
            dve.memset(eps[:], EPS).then_inc(eps_set, 1)
            dve.wait_ge(s_tok, 16)
            dve.tensor_copy(tf[:], tk[:]).then_inc(tok_f, 1)
            dve.wait_ge(s_iota, 16)
            dve.wait_ge(tok_f, 1)
            iot = con("iota").unsqueeze(1).unsqueeze(1).to_broadcast([128, CB, B, NSK])
            qv = cb_view(tf[:, 0, :]).unsqueeze(3).to_broadcast([128, CB, B, NSK])
            rv = cb_view(tf[:, 1, :]).unsqueeze(3).to_broadcast([128, CB, B, NSK])
            dve.tensor_tensor(oh, iot, qv, ALU.is_equal).then_inc(onehot, 1)
            dve.wait_ge(onehot, 1)
            dve.tensor_tensor(ohq, oh, rv, ALU.mult).then_inc(onehot_r, 1)

            def counts(w, i):
                n = min(3, CB - 3 * i)
                dve.wait_ge(cum_ready, 6 * w + i + 1)
                dve.tensor_tensor(prod[:, w, 3 * i:3 * i + n].rearrange("p c b s -> p (c b s)"),
                                  ps[:, 1 + i, 0:n * B * NSK],
                                  oh[:, 3 * i:3 * i + n].rearrange("p c b s -> p (c b s)"), ALU.mult
                                  ).then_inc(cum_used, 1)

            for i in range(6):
                counts(0, i)
            dve.wait_ge(s_w, 16 * 8)
            dve.tensor_reduce(pmean[0:E + 1, 0:1], pt[:, 0:E], AX.X, ALU.add).then_inc(proj_c, 1)
            dve.wait_ge(proj_c, 1)
            dve.tensor_scalar(pmean[0:E + 1, 1:2], pmean[0:E + 1, 0:1], -1.0 / E, None, ALU.mult).then_inc(proj_c, 1)
            dve.wait_ge(proj_c, 2)
            dve.tensor_scalar(pt[:, E:2 * E], pt[:, 0:E], pmean[0:E + 1, 1:2], None, ALU.add).then_inc(proj_c, 1)
            dve.wait_ge(cum_used, 6)
            dve.tensor_reduce(cb_view(ft[:, 1, :]), prod[:, 0], AX.X, ALU.add).then_inc(feat, 1)
            dve.tensor_scalar(val[:, 0, :], tf[:, 0, :], 0.0, None, ALU.is_ge).then_inc(feat, 1)
            dve.wait_ge(feat, 2)
            dve.scalar_tensor_tensor(ft[:, 3, :], tf[:, 0, :], float(NSK), val[:, 0, :], ALU.is_lt, ALU.mult
                                     ).then_inc(feat, 1)
            dve.wait_ge(feat, 3)
            dve.tensor_tensor(ft[:, 0, :], tf[:, 0, :], ft[:, 3, :], ALU.mult).then_inc(feat, 1)
            dve.wait_ge(set1_sb, 1)
            dve.tensor_tensor(wpair[:], w2[:, 0:NF].unsqueeze(2).to_broadcast([E, NF, NF]),
                              w2[:, 0:NF].unsqueeze(1).to_broadcast([E, NF, NF]), ALU.mult).then_inc(pair_ready, 1)
            counts(1, 0)
            counts(1, 1)
            dve.tensor_scalar(val[:, 0, :], ft[:, 1, :], 1.0, None, ALU.max).then_inc(feat, 1)
            dve.wait_ge(feat, 5)
            dve.reciprocal(val[:, 1, :], val[:, 0, :]).then_inc(feat, 1)
            counts(1, 2)
            dve.wait_ge(s_con, 16)
            dve.wait_ge(s_si, 16)
            dve.tensor_tensor(si[:], si[:], con("ident").unsqueeze(1).to_broadcast([HID, NL, HID]), ALU.add
                              ).then_inc(si_ready, 1)
            counts(1, 3)
            dve.wait_ge(cum_used, 9)
            dve.tensor_reduce(cb_view(val[:, 2, :])[:, 0:9], prod[:, 1, 0:9], AX.X, ALU.add).then_inc(feat, 1)
            gp = ps[0:FR, 0, 0:GC]
            dve.wait_ge(set3, 1)
            dve.tensor_copy(gwh[:, 0, :], gp).then_inc(g_step, 1)
            dve.wait_ge(g_step, 1)
            dve.scalar_tensor_tensor(gwr[:], gwh[:, 0, :], con("m36", FR)[:, 0:1], gp, ALU.mult, ALU.add
                                     ).then_inc(g_step, 1)
            counts(1, 4)
            dve.wait_ge(g_step, 2)
            dve.tensor_copy(gwh[:, 1, :], gwr[:]).then_inc(g_step, 1)
            dve.wait_ge(g_step, 3)
            dve.scalar_tensor_tensor(g36[:], gwh[:, 1, :], con("m36", FR)[:, 1:2], gwr[:], ALU.mult, ALU.add
                                     ).then_inc(g_step, 1)
            counts(1, 5)
            dve.wait_ge(cum_used, 12)
            dve.tensor_reduce(cb_view(val[:, 2, :])[:, 9:CB], prod[:, 1, 9:CB], AX.X, ALU.add).then_inc(feat, 1)
            dve.wait_ge(feat, 8)
            dve.tensor_tensor(ft[:, 2, :], val[:, 2, :], val[:, 1, :], ALU.mult).then_inc(feat, 1)
            dve.wait_ge(feat, 9)
            dve.tensor_tensor(outer[:].rearrange("p (f g) c -> p f g c", f=NF),
                              ft.unsqueeze(2).to_broadcast([128, NF, NF, NC]),
                              ft.unsqueeze(1).to_broadcast([128, NF, NF, NC]), ALU.mult).then_inc(ss_ready, 1)
            dve.wait_ge(ss_ready, 1)
            dve.wait_ge(gram_sb, 1)
            dve.tensor_tensor(outg[:], outer[:], gram[:].unsqueeze(2).to_broadcast([128, NF * NF, NC]), ALU.mult
                              ).then_inc(ss_ready, 1)
            dve.wait_ge(ss_ready, 2)
            dve.tensor_reduce(ss[:, 0, :], outg[:].rearrange("p f c -> p c f"), AX.X, ALU.add).then_inc(ss_ready, 1)
            dve.wait_ge(ss_ready, 3)
            dve.tensor_scalar(ss[:, 1, :], ss[:, 0, :], 0.0, EPS, ALU.max, ALU.add).then_inc(ss_ready, 1)

            def in_parts(v, t0):
                fv = f2[:, v, :].rearrange("p (f c) -> p c f", f=NF)
                rv = rest[:, v, :].rearrange("p (f c) -> p c f", f=NF)

                def thrice(ap):
                    return ap.unsqueeze(2).to_broadcast([128, NC, 3, NF])

                dve.tensor_copy(parts[:, v, :, 0], thrice(fv)).then_inc(part_step, 1)
                dve.wait_ge(part_step, t0 + 1)
                dve.tensor_tensor(rv, fv, parts[:, v, :, 0, 0], ALU.subtract).then_inc(part_step, 1)
                dve.wait_ge(part_step, t0 + 2)
                dve.tensor_copy(parts[:, v, :, 1], thrice(rv)).then_inc(part_step, 1)
                dve.wait_ge(part_step, t0 + 3)
                dve.tensor_tensor(parts[:, v, :, 2], thrice(rv), parts[:, v, :, 1], ALU.subtract
                                  ).then_inc(part_step, 1)

            dve.wait_ge(rstd_ready, 2)
            dve.tensor_tensor(ftn, ft, ss[:, 0, :].unsqueeze(1).to_broadcast([128, NF, NC]), ALU.mult
                              ).then_inc(part_step, 1)
            dve.wait_ge(part_step, 1)
            in_parts(1, 1)
            in_parts(0, 5)
            for c0 in range(4):
                dve.wait_ge(fts_ready, c0 + 1)
                dve.tensor_copy(f36[:, 1, c0 * 1024:(c0 + 1) * 1024], ps[0:FR, c0, :].bitcast(BF16)
                                ).then_inc(fts_copied, 1)
            dve.wait_ge(s_late, 16 * 7)
            dve.tensor_tensor(dsum[:], chn("d0"), chn("d1"), ALU.add).then_inc(dsum_ready, 1)
            dve.wait_ge(dsum_ready, 1)
            dve.tensor_scalar(dcen[:], con("cen128"), dsum[:, 0:1], None, ALU.mult).then_inc(dcen_ready, 1)
            dve.tensor_reduce(pmean[:, 2:3], wou[:, 0:E], AX.X, ALU.add).then_inc(wou_step, 1)
            dve.wait_ge(wou_step, 1)
            dve.tensor_scalar(pmean[:, 3:4], pmean[:, 2:3], -1.0 / E, None, ALU.mult).then_inc(wou_step, 1)
            dve.wait_ge(wou_step, 2)
            dve.tensor_scalar(wou[:, E:2 * E], wou[:, 0:E], pmean[:, 3:4], None, ALU.add).then_inc(wou_step, 1)
            dve.tensor_copy(brh[:], br[:]).then_inc(bias_step, 1)
            dve.wait_ge(bias_step, 1)
            dve.scalar_tensor_tensor(brr[:], brh[:], con("mbr", BR)[:, 0:1], br[:], ALU.mult, ALU.add
                                     ).then_inc(bias_step, 1)
            dve.wait_ge(bias_step, 2)
            dve.tensor_copy(brh[:], brr[:]).then_inc(bias_step, 1)
            dve.wait_ge(bias_step, 3)
            dve.scalar_tensor_tensor(brp[:], brh[:], con("mbr", BR)[:, 1:2], brr[:], ALU.mult, ALU.add
                                     ).then_inc(bias_step, 1)
            dve.tensor_scalar(ohr[:], rtb[:], con("eid", BR)[:, 0:1], con("eid", BR)[:, 1:2], ALU.is_equal, ALU.max
                              ).then_inc(bias_step, 1)
            dve.tensor_copy(rtw[:, 0, :], rt[:]).then_inc(route_step, 1)
            dve.wait_ge(route_step, 1)
            dve.tensor_scalar(rtw[:, 1, :], rtw[:, 0, :], 0.0, None, ALU.is_ge).then_inc(route_step, 1)
            dve.wait_ge(route_step, 2)
            dve.scalar_tensor_tensor(rtw[:, 2, :], rtw[:, 0, :], float(NX), rtw[:, 1, :], ALU.is_lt, ALU.mult
                                     ).then_inc(route_step, 1)
            dve.wait_ge(route_step, 3)
            dve.scalar_tensor_tensor(rtw[:, 3, :], rtw[:, 0, :], -float(NX), rtw[:, 2, :], ALU.add, ALU.mult
                                     ).then_inc(route_step, 1)
            dve.wait_ge(route_step, 4)
            dve.tensor_scalar(slot[:], rtw[:, 3, :], float(NX), None, ALU.add).then_inc(route_step, 1)

            for c0 in range(4):
                dve.wait_ge(fts_ready, 4 + c0 + 1)
                dve.tensor_copy(f36[:, 0, c0 * 1024:(c0 + 1) * 1024], ps[0:FR, c0, :].bitcast(BF16)
                                ).then_inc(fts_copied, 1)

            def prep_a(s, it, width, bc, o):
                t = prepared(s, it)
                dve.wait_ge(x_exp, t + 1)
                dve.tensor_scalar(xe[:, o:o + width], xe[:, o:o + width], BIG, None, ALU.min).then_inc(x_min, 1)
                dve.wait_ge(x_hi, t + 1)
                dve.tensor_tensor(xr[:, o:o + width], xh[:, o:o + width], bc, ALU.add).then_inc(x_rest, 1)

            def prep_b(s, it, width, bank, o, dst):
                k = segment(s)[1]
                dve.wait_ge(x_ln, prepared(s, it) + 1)
                dve.scalar_tensor_tensor(dst, bank, chn(f"dt_b{k}"), xl[:, o:o + width], ALU.add, ALU.max
                                         ).then_inc(x_delta, 1)

            for i in range(2):
                prep_a(0, i, HC, ps[0:BCR, 2 * i, :], i * HC)
            for i in range(2):
                prep_b(0, i, HC, ps[:, 1 + 2 * i, :], i * HC, dl[:, 0, i * HC:(i + 1) * HC])
                prep_parts(dve, 0, i, HC, i * HC, i * HC)
            for i in range(2):
                prep_du(dve, 0, i, HC, i * HC, i * HC)

            def product(s, n, j, h, first):
                st = s * N + n
                g = 2 * st + h
                t = phys(segment(s)[1], h) * HC
                dve.wait_ge(scan_done, g + 1)
                dve.wait_ge(c_ready, g + 1)
                if h == 0:
                    opt_ge(dve, sum_done, 2 * (st - UN) + 2, not first)
                dve.tensor_tensor(pv[:, j, t:t + HC], ps[:, 4 + h, :], hv[:, j % 2, t:t + HC], ALU.mult
                                  ).then_inc(p_done, 1)

            def state(s, n, j, middle):
                b, k, c = segment(s)
                start = s % 2 == 0
                st = s * N + n
                first = s == 0 and known(n) and n < UN

                def way(ap):
                    return ap if k == 0 else ap[:, ::-1]

                for h in range(2):
                    g = 2 * st + h
                    t = phys(k, h) * HC
                    if h == 0:
                        opt_ge(dve, p_done, 2 * st - 2, not (s == 0 and known(n) and n < 2))
                        dve.wait_ge(mul_done, st + 1)
                        initial = 0.0 if start else carry[:, ds(n, 1)]
                    else:
                        e = phys(k, 0) * HC + (HC - 1 if k == 0 else 0)
                        initial = hv[:, j % 2, e:e + 1]
                        dve.wait_ge(scan_done, g)
                    dve.wait_ge(a_ready, g + 1)
                    dve.tensor_tensor_scan(way(hv[:, j % 2, t:t + HC]), way(ps[:, 2 + h, :]),
                                           way(bv[:, j, t:t + HC]), initial, ALU.mult, ALU.add).then_inc(scan_done, 1)
                    if h == 1:
                        product(s, n, j, 0, first)
                    elif known(n) and n == 0:
                        if s > 0:
                            product(s - 1, N - 1, UN - 1, 1, False)
                    else:
                        product(s, n - 1, (j - 1) % UN, 1, first)
                    if h == 0:
                        middle()

            def first_normed(q):
                dve.wait_ge(q_rs2, q + 1)
                dve.tensor_tensor(hn0[E:128, :], h0[E:128, :], rs0[E:128, :], ALU.mult).then_inc(q_hn, 1)

            def early(n):
                for q in range(2):
                    step = n - 8 * q
                    if step == 2:
                        dve.wait_ge(q_rs, q + 1)
                        dve.scalar_tensor_tensor(tt0, u[:, q * HC:(q + 1) * HC], chn("ln_w"), rs0, ALU.mult, ALU.mult
                                                 ).then_inc(q_t1, 1)
                    elif step == 3:
                        dve.wait_ge(q_t1, q + 1)
                        dve.scalar_tensor_tensor(tt0, tt0, chn("ln_b"), z[:, q * HC:(q + 1) * HC], ALU.add, ALU.mult
                                                 ).then_inc(q_t, 1)
                if n == 8:
                    first_normed(0)

            def turn(s, it):
                nx = s + 1
                if nx < NSEG:
                    nk = segment(nx)[1]
                    local = snapped(dve, it * SL if nk == 0 else it * -SL + (IT - 1) * SL)
                for j in range(UN):
                    def middle():
                        if j == 0 and nx < NSEG:
                            prep_a(nx, it, SL, ps[0:BCR, 6, 0:SL], 0)

                    state(s, it * UN + j, j, middle)
                    if s == NSEG - 1:
                        early(it * UN + j)
                    if j == 0 and nx < NSEG:
                        prep_b(nx, it, SL, ps[:, 6, SL:2 * SL], 0, dl[:, nx % 2, ds(local, SL)])

            for s in range(NSEG):
                turn(s, 0)
                if s < NSEG - 1:
                    with dve.Fori(1, IT) as it:
                        turn(s, it)
                else:
                    for it in range(1, IT):
                        turn(s, it)
            product(NSEG - 1, N - 1, UN - 1, 1, False)

            def gated(qq):
                for p in range(2):
                    q = 2 * qq + p
                    dve.wait_ge(q_rs, q + 1)
                    dve.scalar_tensor_tensor(tt[:, p, :], u[:, ds(q * HC, HC)], chn("ln_w"), rs[:, p, :],
                                             ALU.mult, ALU.mult).then_inc(q_t1, 1)
                for p in range(2):
                    q = 2 * qq + p
                    dve.wait_ge(q_t1, q + 1)
                    dve.scalar_tensor_tensor(tt[:, p, :], tt[:, p, :], chn("ln_b"), z[:, ds(q * HC, HC)],
                                             ALU.add, ALU.mult).then_inc(q_t, 1)

            def normed(qq):
                for p in range(2):
                    dve.wait_ge(q_rs2, 2 * qq + p + 1)
                    dve.tensor_tensor(hn[E:128, p, :], ps[E:128, bank_h1[p], :], rs[E:128, p, :], ALU.mult
                                      ).then_inc(q_hn, 1)

            def result(qq):
                for p in range(2):
                    q = 2 * qq + p
                    h = z[0:E, ds(q * HC, HC)]
                    dve.wait_ge(q_wo, q + 1)
                    dve.scalar_tensor_tensor(h, ps[0:E, bank_ffn[p], :], chn("bo", E), h, ALU.add, ALU.add
                                             ).then_inc(q_out, 1)

            first_normed(1)
            with dve.Fori(0, Q // 2 - 1) as qq:
                gated(qq + 1)
                normed(qq + 1)
                result(qq)
            result(Q // 2 - 1)

        @block.tensor
        def _(pe):
            def totals(data, ones, col):
                for i in range(CB):
                    m = pe.matmul(ps[0:CB, 0, col:col + B * NSK], ones[:, i * CB:(i + 1) * CB],
                                  data[:, i].rearrange("p b s -> p (b s)"), start=(i == 0), stop=(i == CB - 1))
                m.then_inc(tot_ready, 1)

            def counts(w, g):
                t_in, m_in, data, before = ((cbn("tri"), cm, oh, tot), (con("tri"), cmf, ohq, totr))[w]
                if w == 1:
                    pe.wait_ge(cum_used, g + 1)
                for i in range(3 * g, min(3 * g + 3, CB)):
                    dst = ps[:, 1 + g, (i % 3) * B * NSK:(i % 3 + 1) * B * NSK]
                    pe.matmul(dst, t_in, data[:, i].rearrange("p b s -> p (b s)"), start=True, stop=False)
                    m = pe.matmul(dst, m_in[:, i * 128:(i + 1) * 128], before[:], start=False, stop=True)
                m.then_inc(cum_ready, 1)

            pe.wait_ge(s_cb, 16)
            pe.wait_ge(onehot, 1)
            totals(oh, cbn("ind"), 0)
            pe.wait_ge(s_cm, 16)
            pe.wait_ge(tot_sb, 1)
            for g in range(6):
                counts(0, g)
            pe.wait_ge(s_con, 16)
            pe.wait_ge(onehot_r, 1)
            totals(ohq, con("indf"), 256)
            pe.wait_ge(s_w, 16 * 8)
            pe.wait_ge(proj_c, 3)
            pe.matmul(ps[0:E, 7, W2], pt[:, E:2 * E], tm[:], start=True, stop=True)
            for k in range(K):
                at = WDT.start + k * DI
                m = pe.matmul(ps[:, 7, at:at + DI], xd[:, k, :], dw[:, k, :], start=True, stop=True)
            m.then_inc(set1, 1)
            pe.wait_ge(tot_sb, 2)
            pe.wait_ge(cmf_ready, 1)
            counts(1, 0)
            counts(1, 1)
            pe.wait_ge(set1_sb, 2)
            pe.wait_ge(pair_ready, 1)
            pe.matmul(ps[:, 7, GX], win[:, 0:DI], w2[:], start=True, stop=True)
            pe.matmul(ps[:, 7, GRAM], con("one64", E), wpair[:].rearrange("p f g -> p (f g)"),
                      start=True, stop=True).then_inc(set2, 1)
            counts(1, 2)
            counts(1, 3)
            pe.wait_ge(set2_sb, 1)
            pe.matmul(ps[0:FR, 0, 0:128], tm[:], pt[:], start=True, stop=True)
            pe.matmul(ps[0:FR, 0, 128:128 + DI], gx[:], cvt[:], start=True, stop=True)
            pe.matmul(ps[0:FR, 0, 128 + DI:128 + 2 * DI], w2[:], win[:, DI:2 * DI], start=True, stop=True
                      ).then_inc(set3, 1)
            counts(1, 4)
            counts(1, 5)

            def parts_t(v, c0):
                for i in range(8):
                    m = pe.transpose(ps[0:FR, c0, :].bitcast(BF16)[:, i * 128:(i + 1) * 128],
                                     parts[:, v, 8 * c0 + i].rearrange("p i j f -> p (i j f)"), cbn("ident"))
                m.then_inc(fts_ready, 1)

            pe.wait_ge(part_step, 5)
            pe.wait_ge(g_step, 4)
            pe.wait_ge(cum_used, 12)
            pe.wait_ge(gram_sb, 1)
            for c0 in range(4):
                parts_t(1, c0)
            for w in range(2):
                wt = g36[:, 128 + w * DI:128 + (w + 1) * DI]
                for i in range(Q):
                    if w == 0 and i % 2 == 0:
                        pe.wait_ge(fts_copied, i // 2 + 1)
                    opt_ge(pe, xz_done, w * Q + i - 3, w * Q + i > 3)
                    pe.matmul(ps[:, 4 + i % 4, :], wt, f36[:, 1, i * HC:(i + 1) * HC], start=True, stop=True
                              ).then_inc(xz_ready, 1)
                    if w * Q + i in (3, 5, 7, 9):
                        c0 = (w * Q + i - 3) // 2
                        pe.wait_ge(part_step, 9)
                        pe.wait_ge(fts_copied, c0 + 1)
                        parts_t(0, c0)

            def prep(s, u_ap, bc, dt):
                k = segment(s)[1]
                pe.matmul(bc, xb[:, k, :], u_ap, start=True, stop=True)
                pe.matmul(dt, wdt[:, k, :], u_ap, start=True, stop=True).then_inc(x_ready, 1)

            for i in range(2):
                pe.wait_ge(fts_copied, 6 + 2 * i)
                prep(0, u[:, i * HC:(i + 1) * HC], ps[0:BCR, 2 * i, :], ps[:, 1 + 2 * i, :])

            def spread(s, n, h, bank, which, ready):
                s, n = (s + 1, n - N) if known(n) and n >= N else (s, n)
                k = segment(s)[1]
                t = phys(k, h) * HC
                pe.matmul(ps[:, bank, :], selb[0:BCR, ds(which * N + n, 1), :].rearrange("p o d -> p (o d)"),
                          pr[:, s % 2, t:t + HC], start=True, stop=True).then_inc(ready, 1)

            def spread_c(s, n, h):
                g = 2 * (s * N + n) + h
                opt_ge(pe, p_done, g - 1, not (s == 0 and known(n) and n == 0))
                spread(s, n, h, 4 + h, 1, c_ready)

            def add_up(s, n, j, w, stop=False):
                st = s * N + n
                if w == 0:
                    pe.wait_ge(p_done, 2 * st + 2)
                pe.matmul(ps[:, w, :], con("cen128"), pv[:, j, w * HC:(w + 1) * HC], start=False, stop=stop
                          ).then_inc(sum_done, 1)

            def begin_y(s, w):
                b, k, c = segment(s)
                t = b * L + c * CH + w * HC
                opt_ge(pe, y_taken, 2 * ((0, 1, 0, 2)[s % 4] + 3 * (s // 4)) - 1 + w, s > 0)
                if k == 0:
                    pe.matmul(ps[:, w, :], dcen[:], u[:, t:t + HC], start=True, stop=False)
                else:
                    pe.matmul(ps[:, w, :], con("ident"), ysv[:, w * HC:(w + 1) * HC], start=True, stop=False)

            def var(qq):
                for p in range(2):
                    pe.wait_ge(q_sq, 2 * qq + p + 1)
                    pe.matmul(ps[:, bank_var[p], :], con("one128"), sq[:, p, :], start=True, stop=True
                              ).then_inc(q_var, 1)

            def attention_out(qq):
                for p in range(2):
                    q = 2 * qq + p
                    pe.wait_ge(q_t, q + 1)
                    pe.matmul(ps[:, bank_h1[p], :], wou[:], tt[:, p, :], start=True, stop=False)
                    pe.matmul(ps[:, bank_h1[p], :], g36[:, 0:128], f36[:, 0, ds(q * HC, HC)], start=False, stop=True
                              ).then_inc(q_o, 1)

            def var2(qq):
                for p in range(2):
                    pe.wait_ge(q_sq2, 2 * qq + p + 1)
                    pe.matmul(ps[:, bank_var[p], :], con("one64")[E:128, :], sq[E:128, p, :], start=True, stop=True
                              ).then_inc(q_var2, 1)

            def ffn_in(qq):
                for p in range(2):
                    pe.wait_ge(q_hn, 2 * qq + p + 1)
                    pe.matmul(ps[:, bank_in[p], :], wi_[E:128, :], hn[E:128, p, :], start=True, stop=True
                              ).then_inc(q_w, 1)

            def first_ffn_in(q):
                pe.wait_ge(q_hn, q + 1)
                pe.matmul(ps[:, (6, 4)[q], :], wi_[E:128, :], hn0[E:128, :], start=True, stop=True).then_inc(q_w, 1)

            def early(n):
                for q in range(2):
                    step = n - 8 * q
                    if step == 1:
                        pe.wait_ge(q_sq, q + 1)
                        pe.matmul(ps[:, 6, :], con("one128"), sq0, start=True, stop=True).then_inc(q_var, 1)
                    elif step == 5:
                        pe.wait_ge(q_t, q + 1)
                        pe.wait_ge(wou_step, 3)
                        pe.matmul(ps[:, 6, :], wou[:], tt0, start=True, stop=False)
                        pe.matmul(ps[:, 6, :], g36[:, 0:128], f36[:, 0, q * HC:(q + 1) * HC], start=False, stop=True
                                  ).then_inc(q_o, 1)
                    elif step == 7:
                        pe.wait_ge(q_sq2, q + 1)
                        pe.matmul(ps[:, 6, :], con("one64")[E:128, :], sq0[E:128, :], start=True, stop=True
                                  ).then_inc(q_var2, 1)
                if n == 10:
                    pe.wait_ge(q_ln, 2)
                    first_ffn_in(0)

            def layer(l, qq, p):
                q = 2 * qq + p
                src, ready, done = ((fa, q_f0, q_l0), (fb, q_f1, q_l1))[l]
                if known(qq) and qq == 0 and l == 0:
                    src = fa0
                bank = bank_ffn[p]
                if l == 0:
                    if not isinstance(qq, int) or qq > 0:
                        pe.wait_ge(q_out, q - 1)
                    for half in range(2):
                        pe.wait_ge(we_loaded[p][half], 16 * (GQ // 2) * (qq + 1))
                pe.wait_ge(ready, q + 1)
                pe.matmul(ps[:, bank, :].rearrange("p (g t) -> p g t", t=TG), brp[:, l * HID:(l + 1) * HID],
                          ohr[:, ds(q * GQ, GQ)].unsqueeze(2).to_broadcast([BR, GQ, TG]), start=True, stop=False)
                for g in range(GQ):
                    m = pe.matmul(ps[:, bank, g * TG:(g + 1) * TG], we[:, p * GQ + g, l, :],
                                  src[:, p, g * TG:(g + 1) * TG], start=False, stop=(g == GQ - 1))
                m.then_inc(done, 1)

            def ffn_out(qq):
                for p in range(2):
                    pe.wait_ge(q_f2, 2 * qq + p + 1)
                    pe.matmul(ps[:, bank_ffn[p], :], wo_[:], fc[:, p, :], start=True, stop=True).then_inc(q_wo, 1)

            def both(qq):
                layer(0, qq, 0)
                layer(0, qq, 1)
                layer(1, qq, 0)
                attention_out(qq + 1)
                layer(1, qq, 1)
                var2(qq + 1)
                ffn_out(qq)
                if qq + 2 < Q // 2:
                    pe.wait_ge(q_ln2, 2 * qq + 4)
                    var(qq + 2)
                ffn_in(qq + 1)

            def turn(s, it):
                nx = s + 1
                for j in range(UN):
                    n = it * UN + j
                    if j == 0 and nx < NSEG:
                        nb, nk, nc_ = segment(nx)
                        local = snapped(pe, it * SL if nk == 0 else it * -SL + (IT - 1) * SL)
                        pe.wait_ge(x_delta, prepared(nx, it))
                        if known(it) and it == 0 and s == 0:
                            pe.wait_ge(b_copied, 4)
                        prep(nx, u[:, ds(nb * L + nc_ * CH + local, SL)], ps[0:BCR, 6, 0:SL], ps[:, 6, SL:2 * SL])
                    for h in range(2):
                        g = 2 * (s * N + n) + h
                        if not known(it) or it > 0:
                            add_up(s, n - 3, (j + 1) % UN, h)
                        elif j == 3:
                            if s > 0 and s % 4 != 2:
                                begin_y(s, h)
                            add_up(s, 0, 0, h)
                        elif s > 0:
                            add_up(s - 1, N - 3 + j, 1 + j, h, j == 2 and (s - 1) % 4 != 1)
                        if h == 1:
                            spread_c(s, n, 0)
                        elif not known(n) or n > 0:
                            spread_c(s, n - 1, 1)
                        elif s > 0:
                            spread_c(s - 1, N - 1, 1)
                        if not (s == NSEG - 1 and known(n) and n + 2 + h >= N):
                            if known(n) and n + 3 == N and h == 1:
                                pe.wait_ge(x_parts, prepared(s + 2, 0))
                            pe.wait_ge(b_copied, g + 5)
                            spread(s, n + 2 + h, 1 - h, 7, 0, b_ready)
                    if s == NSEG - 1:
                        early(n)

            pe.wait_ge(x_delta, 1)
            pe.wait_ge(dcen_ready, 1)
            for w in range(2):
                begin_y(0, w)
            pe.wait_ge(sel_ready, 1)
            pe.wait_ge(x_parts, 2)
            for g in range(5):
                if g == 4:
                    pe.wait_ge(b_copied, 1)
                elif g == 0:
                    pe.wait_ge(xz_done, 2 * Q)
                spread(0, g // 2, g % 2, 7 - g % 4, 0, b_ready)
            pe.wait_ge(x_delta, 2)
            for s in range(NSEG):
                turn(s, 0)
                if s < NSEG - 1:
                    with pe.Fori(1, IT - 1) as it:
                        turn(s, it)
                else:
                    for it in range(1, IT - 1):
                        turn(s, it)
                turn(s, IT - 1)
            spread_c(NSEG - 1, N - 1, 1)
            for j in (1, 2, 3):
                for w in range(2):
                    add_up(NSEG - 1, N - UN + j, j, w, j == 3)

            pe.wait_ge(bias_step, 5)
            first_ffn_in(1)
            var(1)
            for qq in range(Q // 2 - 1):
                both(qq)
            for l in range(2):
                for p in range(2):
                    layer(l, Q // 2 - 1, p)
            ffn_out(Q // 2 - 1)


def constants():
    import numpy as np
    cf = np.zeros((128, CFW), np.float32)

    def put(name, a):
        cf[:a.shape[0], CF[name][0]:CF[name][0] + a.shape[1]] = a

    i = np.arange(128)
    eye = np.eye(128, dtype=np.float32)
    put("ident", eye)
    put("tri", (i[:, None] <= i[None, :]).astype(np.float32))
    put("cen128", eye - np.float32(1 / DI))
    put("one128", np.full((128, 128), 1 / DI, np.float32))
    put("one64", np.full((128, 128), 1 / E, np.float32))
    put("iota", np.tile(np.arange(NSK, dtype=np.float32), (128, 1)))

    def part_masks(part):
        return np.stack([-1.0 * (part >= 1), -1.0 * (part >= 2)], 1).astype(np.float32)

    put("m36", part_masks(np.arange(FR) // NF % 3))
    r = np.arange(BCR)
    put("mbc", part_masks((r % 64) // N))
    r = np.arange(BR)
    put("mbr", part_masks(r // 32))
    e = r % 32
    put("eid", np.stack([np.where(e < NX, e, -1e9), 1.0 * (e == NX)], 1).astype(np.float32))
    put("indf", np.tile(np.eye(CB, dtype=np.float32).reshape(1, -1), (128, 1)))
    sel = np.zeros((128, 2 * N), np.float32)
    for w in range(2):
        for n in range(N):
            for part in range(3):
                sel[64 * w + part * N + n, w * N + n] = 1.0
    put("sel", sel)
    cm = (np.arange(CB)[:, None, None] < np.arange(CB)[None, :, None]) * np.ones((1, 1, 128))
    cb = np.concatenate([cf[:, slice(*CF[n])] for n in ("tri", "indf", "ident")], 1)
    one = 0x3F80
    return cf, (cb * one).astype(np.uint16), (cm.reshape(CB, CB * 128) * one).astype(np.uint16)


def kernel(**inputs):
    import numpy as np
    import concourse.bacc as _bacc
    from concourse.bass_utils import run_bass_kernel_spmd as _run

    x = {n: np.asarray(v) for n, v in inputs.items()}
    a = {n[8:]: v for n, v in x.items() if n.startswith("L0_attn_")}
    f = {n[7:]: v for n, v in x.items() if n.startswith("L0_ffn_")}
    t = {n[7:]: v for n, v in x.items() if n.startswith("L0_tok_")}
    f32 = np.float32

    def toks(v):
        return v.reshape(B, CB, 128).transpose(2, 0, 1).reshape(128, NC)

    def col(v):
        return np.concatenate([v, np.zeros(128 - v.shape[0], f32)])

    cf, cb, cm = constants()
    m = np.zeros((E + 1, NF), f32)
    n0, n1 = t["skill_w"].shape[0], t["skill_w"].shape[0] + t["att_w"].shape[0]
    m[0:n0, 0], m[n0:n1, 1], m[n1:E, 2] = t["skill_w"], t["att_w"], t["mast_w"]
    m[0:n0, 3], m[n0:n1, 3], m[n1:E, 3] = t["skill_b"], t["att_b"], t["mast_b"]
    m[E, 3] = 1.0
    xp = a["x_proj_w"]
    xbc = np.zeros((DI, K, BCR), f32)
    for part in range(3):
        xbc[:, :, part * N:(part + 1) * N] = xp[:, R:R + N].transpose(2, 0, 1)
        xbc[:, :, 64 + part * N:64 + (part + 1) * N] = xp[:, R + N:R + 2 * N].transpose(2, 0, 1)
    bb = np.concatenate([f["br"].transpose(1, 0, 2), f["bs"].transpose(1, 0, 2)], 0).reshape(NX + 1, NL * HID)
    route = f["route_id"].reshape(1, NR)
    arrays = {
        "tok": np.stack([toks(x["x"]), toks(x["mask_BS_i0_1"])], 1),
        "consts": cf, "constb": cb, "cmask": cm,
        "chan": np.stack([a["conv_b"], a["dt_b"][0], a["dt_b"][1], a["Ds"][:DI], a["Ds"][DI:], a["ln_w"], a["ln_b"],
                          f["bi"], col(f["bo"])], 1),
        "tokm": np.tile(m, (1, FR // NF)),
        "projt": np.pad(np.concatenate([t["proj_w"].T, t["proj_b"][None]], 0), ((0, 0), (0, 128 - E))),
        "wint": a["W_in"].T, "convt": a["conv_w"].T, "xbc": xbc,
        "xdt": xp[:, :R].transpose(1, 0, 2), "dtw": a["dt_w"].transpose(2, 0, 1),
        "alog": a["A_logs"].reshape(K, DI, N).transpose(1, 0, 2).reshape(DI, K * N),
        "wout": np.pad(a["W_out"].T, ((0, 0), (0, 128 - E))), "wit": np.pad(f["Wi"].T, ((128 - E, 0), (0, 0))),
        "ws": f["Ws"][:, 0].transpose(2, 0, 1), "wo": np.pad(f["Wo"].T, ((0, 0), (0, 128 - E))),
        "wr": f["Wr"].transpose(1, 3, 0, 2), "brb": np.tile(np.pad(bb, ((0, 31 - NX), (0, 0))), (3, 1)),
        "route": route, "routeb": np.tile(route, (BR, 1)),
    }
    arrays = {n: np.ascontiguousarray(v) for n, v in arrays.items()}
    nc = _bacc.Bacc("TRN2", target_bir_lowering=False, num_devices=1)
    args = [nc.dram_tensor(n, v.shape, mybir.dt.from_np(v.dtype), kind="ExternalInput").ap()
            for n, v in arrays.items()]
    args.append(nc.dram_tensor("wsum", (NX + 1, HID, NL, HID), F32, kind="Internal").ap())
    args.append(nc.dram_tensor("h_t", (E, T), F32, kind="ExternalOutput").ap())
    bass_lm_tower(nc, *args)
    r = _run(nc, [arrays], core_ids=[0])
    return np.ascontiguousarray(r.results[0]["h_t"].T).reshape(B, L, E)
```
